# Optimizing a Trainium2 kernel written in Bass

```python
import numpy as np
import jax
import jax.numpy as jnp

def _softmax(x, axis=-1):
    return jax.nn.softmax(x, axis=axis)

def _gelu(x):
    return jax.nn.gelu(x, approximate=True)

def _silu(x):
    return jax.nn.silu(x)

def _sigmoid(x):
    return jax.nn.sigmoid(x)

def _layernorm(x, axis=-1, eps=1e-05):
    m = jnp.mean(x, axis=axis, keepdims=True)
    v = jnp.var(x, axis=axis, keepdims=True)
    return (x - m) / jnp.sqrt(v + eps)

def _scatter_add(tgt, idx, src, axis=0):
    return tgt.at[idx].add(src)

def _segment_sum(src, seg, n):
    return jax.ops.segment_sum(src, seg, n)
kernel_name = 'mk_xattn_ffn_d1_seqx_r2_cab811'

def setup_inputs(seed: int=0):
    np.random.seed(seed)
    _w = jnp.asarray

    def _rec_inputs():
        import jax
        import jax.numpy as jnp
        _rk = jax.random.key(seed)
        x = -0.0002928 + 1 * jax.random.normal(jax.random.fold_in(_rk, 1), (8, 100, 512), jnp.float32)
        _lenS = 100 - jax.random.randint(jax.random.fold_in(_rk, 7), (8,), 0, max(1, 100 // 4) + 1, jnp.int32)
        _lenS2 = 722 - jax.random.randint(jax.random.fold_in(_rk, 8), (8,), 0, max(1, 722 // 4) + 1, jnp.int32)
        _ctx_1024P = jax.random.normal(jax.random.fold_in(_rk, 11), (8, 16, 512), jnp.float32)
        _ctx_1024c = jax.random.dirichlet(jax.random.fold_in(_rk, 511), 0.3 * jnp.ones((16,), jnp.float32), (8, 722))
        _ctx_1024t = jnp.einsum('bsk,bkd->bsd', _ctx_1024c, _ctx_1024P)
        _ctx_1024t = _ctx_1024t * jax.lax.rsqrt(jnp.mean(jnp.square(_ctx_1024t)) + 1e-12) * 0.953939
        ctx_1024 = -1.39393e-06 + 0.999914 * (_ctx_1024t + 0.3 * jax.random.normal(jax.random.fold_in(_rk, 611), (8, 722, 512), jnp.float32))
        return (x, ctx_1024)
    x, ctx_1024 = _rec_inputs()

    def _L0_xattn_setup():
        import jax, jax.numpy as jnp
        import numpy as np
        D_MODEL = 512
        N_HEADS = 16
        HEAD_DIM = D_MODEL // N_HEADS

        def sparsemax(x):
            x = x - jnp.max(x, axis=-1, keepdims=True)
            zs = -jnp.sort(-x, axis=-1)
            L = x.shape[-1]
            rho = jnp.arange(1, L + 1, dtype=x.dtype)
            cssv = jnp.cumsum(zs, axis=-1) - 1.0
            support = zs > cssv / rho
            k = jnp.maximum(jnp.sum(support, axis=-1, keepdims=True), 1)
            tau = jnp.take_along_axis(cssv, k - 1, axis=-1) / k.astype(x.dtype)
            return jnp.clip(x - tau, 0.0)

        def _split_heads(x):
            B, L, _ = x.shape
            return x.reshape(B, L, N_HEADS, HEAD_DIM).transpose(0, 2, 1, 3)
        key = jax.random.key(seed)
        ks = jax.random.split(key, 11)
        B, L = (2, 1024)
        s = 0.02
        inp = {'q': jax.random.normal(ks[0], (B, L, D_MODEL), jnp.float32), 'k': jax.random.normal(ks[1], (B, L, D_MODEL), jnp.float32), 'v': jax.random.normal(ks[2], (B, L, D_MODEL), jnp.float32), 'Wq': jax.random.normal(ks[3], (D_MODEL, D_MODEL), jnp.float32) * s, 'bq': jnp.zeros((D_MODEL,), jnp.float32), 'Wk': jax.random.normal(ks[4], (D_MODEL, D_MODEL), jnp.float32) * s, 'bk': jnp.zeros((D_MODEL,), jnp.float32), 'Wv': jax.random.normal(ks[5], (D_MODEL, D_MODEL), jnp.float32) * s, 'bv': jnp.zeros((D_MODEL,), jnp.float32), 'Wo': jax.random.normal(ks[6], (D_MODEL, D_MODEL), jnp.float32) * s, 'bo': jnp.zeros((D_MODEL,), jnp.float32)}
        return inp
    _L0_xattn_all = _L0_xattn_setup()
    _L0_xattn_in = {k: v for k, v in _L0_xattn_all.items() if k in ('Wq', 'bq', 'Wk', 'bk', 'Wv', 'bv', 'Wo', 'bo')}
    del _L0_xattn_all

    def _L0_ffn_setup():
        import jax, jax.numpy as jnp
        import numpy as np
        INPUT_SIZE = 512
        OUTPUT_SIZE = 512
        key = jax.random.key(seed)
        kx, kt, kp, ktn, kpn = jax.random.split(key, 5)
        x = jax.random.normal(kx, (8, 1024, INPUT_SIZE), dtype=jnp.float32)
        theta = jax.random.normal(kt, (INPUT_SIZE, OUTPUT_SIZE), dtype=jnp.float32) * 0.02
        phi = jax.random.normal(kp, (INPUT_SIZE, OUTPUT_SIZE), dtype=jnp.float32) * 0.02
        theta_noise = jax.random.normal(ktn, (INPUT_SIZE, OUTPUT_SIZE), dtype=jnp.float32) * 0.01
        phi_noise = jax.random.normal(kpn, (INPUT_SIZE, OUTPUT_SIZE), dtype=jnp.float32) * 0.01
        return {'x': x, 'theta': theta, 'phi': phi, 'theta_noise': theta_noise, 'phi_noise': phi_noise}
    _L0_ffn_all = _L0_ffn_setup()
    _L0_ffn_in = {k: v for k, v in _L0_ffn_all.items() if k in ('theta', 'phi', 'theta_noise', 'phi_noise')}
    del _L0_ffn_all
    return {'x': x, 'ctx_1024': ctx_1024, 'L0_xattn_Wq': _L0_xattn_in['Wq'], 'L0_xattn_bq': _L0_xattn_in['bq'], 'L0_xattn_Wk': _L0_xattn_in['Wk'], 'L0_xattn_bk': _L0_xattn_in['bk'], 'L0_xattn_Wv': _L0_xattn_in['Wv'], 'L0_xattn_bv': _L0_xattn_in['bv'], 'L0_xattn_Wo': _L0_xattn_in['Wo'], 'L0_xattn_bo': _L0_xattn_in['bo'], 'L0_ffn_theta': _L0_ffn_in['theta'], 'L0_ffn_phi': _L0_ffn_in['phi'], 'L0_ffn_theta_noise': _L0_ffn_in['theta_noise'], 'L0_ffn_phi_noise': _L0_ffn_in['phi_noise']}

def reference(x, ctx_1024, L0_xattn_Wq, L0_xattn_bq, L0_xattn_Wk, L0_xattn_bk, L0_xattn_Wv, L0_xattn_bv, L0_xattn_Wo, L0_xattn_bo, L0_ffn_theta, L0_ffn_phi, L0_ffn_theta_noise, L0_ffn_phi_noise):
    import jax
    import jax.numpy as jnp

    def _L0_xattn_ref(q, k, v, Wq, bq, Wk, bk, Wv, bv, Wo, bo):
        import jax, jax.numpy as jnp
        import numpy as np
        D_MODEL = 512
        N_HEADS = 16
        HEAD_DIM = D_MODEL // N_HEADS

        def sparsemax(x):
            x = x - jnp.max(x, axis=-1, keepdims=True)
            zs = -jnp.sort(-x, axis=-1)
            L = x.shape[-1]
            rho = jnp.arange(1, L + 1, dtype=x.dtype)
            cssv = jnp.cumsum(zs, axis=-1) - 1.0
            support = zs > cssv / rho
            k = jnp.maximum(jnp.sum(support, axis=-1, keepdims=True), 1)
            tau = jnp.take_along_axis(cssv, k - 1, axis=-1) / k.astype(x.dtype)
            return jnp.clip(x - tau, 0.0)

        def _split_heads(x):
            B, L, _ = x.shape
            return x.reshape(B, L, N_HEADS, HEAD_DIM).transpose(0, 2, 1, 3)
        qh = _split_heads(q @ Wq + bq)
        kh = _split_heads(k @ Wk + bk)
        vh = _split_heads(v @ Wv + bv)
        scale = HEAD_DIM ** (-0.5)
        scores = jnp.einsum('bhqd,bhkd->bhqk', qh, kh) * scale
        attn = sparsemax(scores)
        out = jnp.einsum('bhqk,bhkd->bhqd', attn, vh)
        B, L = (q.shape[0], q.shape[1])
        out = out.transpose(0, 2, 1, 3).reshape(B, L, D_MODEL)
        return out @ Wo + bo

    def _L0_ffn_ref(x, theta, phi, theta_noise, phi_noise):
        import jax, jax.numpy as jnp
        import numpy as np
        INPUT_SIZE = 512
        OUTPUT_SIZE = 512
        real = jnp.einsum('bti,io->bto', x, jnp.cos(theta + theta_noise))
        imag = jnp.einsum('bti,io->bto', x, jnp.sin(phi + phi_noise))
        return jnp.sqrt(real * real + imag * imag)
    x = x + _L0_xattn_ref(_layernorm(x, axis=-1), ctx_1024, ctx_1024, L0_xattn_Wq, L0_xattn_bq, L0_xattn_Wk, L0_xattn_bk, L0_xattn_Wv, L0_xattn_bv, L0_xattn_Wo, L0_xattn_bo)
    x = x + _L0_ffn_ref(_layernorm(x, axis=-1), L0_ffn_theta, L0_ffn_phi, L0_ffn_theta_noise, L0_ffn_phi_noise)
    return x

_drawn_inputs = setup_inputs


def setup_inputs(seed=0):
    import zlib

    import numpy as np

    out = dict(_drawn_inputs(seed))
    spreads = {'L0_xattn_bq': (0.0, 0.1),
     'L0_xattn_bk': (0.0, 0.8),
     'L0_xattn_bv': (0.0, 0.1),
     'L0_xattn_bo': (0.0, 0.1)}
    factors = {'L0_ffn_theta': 8.0, 'L0_ffn_theta_noise': 8.0}
    for name, (base, spread) in spreads.items():
        noise = np.random.default_rng([zlib.crc32(name.encode()), seed]).standard_normal(out[name].shape)
        drawn = base * np.exp(spread * noise) if base else spread * noise
        out[name] = jnp.asarray(drawn.astype(out[name].dtype))
    for name, factor in factors.items():
        out[name] = (out[name] * factor).astype(out[name].dtype)
    return out
```

```python
from contextlib import ExitStack

import concourse.bass as bass
from concourse import mybir

F32 = mybir.dt.float32
BF16 = mybir.dt.bfloat16
I32 = mybir.dt.int32
ALU = mybir.AluOpType
ACT = mybir.ActivationFunctionType
AX = mybir.AxisListType.X

P = 128
TWO_PI = 6.283185307179586
TWO_PI_HI = 6.28125
TWO_PI_LO = TWO_PI - TWO_PI_HI
ROUND = 1.5 * 2.0 ** 23
PI_BELOW = 3.1415925
LN_EPS = 1e-5
SUM_TOL = 1e-5
TOP = 40
PIECES = 12
NEWTON_MAX = 28
LOWEST = -3.0e38


class Ring:

    def __init__(self, per_pass):
        self.n, self.per_pass, self.passes = 0, per_pass, 0

    def take(self):
        n = self.n
        self.n += 1
        return n % 2, n, n + self.passes * self.per_pass if self.per_pass else n


def build_kernel(nc, x, ctx_in, Wq, bq, Wk, bk, Wv, bv, Wo, bo, theta, phi, theta_noise, phi_noise, out):
    B, L, D = x.shape
    N = ctx_in.shape[1]
    H = 16
    DH = D // H
    DC = D // P
    G = H // DC
    NC = -(-N // P)
    LAST = N - (NC - 1) * P
    HALF = N // 2
    TH = NC // 2 * L
    SCALE = float(DH) ** -0.5
    NCAND = 8 * PIECES
    cuts = [N * i // PIECES for i in range(PIECES + 1)]
    USES = H + 1 + NC // 2 + 1 + 1 + NC // 2 + 1 + DC

    assert D == DC * P and H == DC * G and N == 2 * HALF and NC % 2 == 0 and USES % 2 == 0

    es = ExitStack()
    with es:
        def sb(name, shape, dt=F32):
            return es.enter_context(nc.sbuf_tensor(name, shape, dt))

        def sem(name):
            return es.enter_context(nc.semaphore(name))

        wq, wk, wv, wo = (sb(n, [P, DC, D]) for n in ("wq", "wk", "wv", "wo"))
        wcos, wsin = sb("wcos", [P, DC, D]), sb("wsin", [P, DC, D])
        ctx_nat = sb("ctx_nat", [P, NC, D])
        ctxT = sb("ctxT", [P, DC, NC * P])
        kT = sb("kT", [P, DC, N])
        v = sb("v", [P, NC, D])
        S = sb("S", [P, H, NC * P])
        pT = sb("pT", [P, G, NC * L])
        qz = sb("qz", [P, DC, G, L])
        q_raw = sb("q_raw", [P, DC, L])
        aT = sb("aT", [P, DC, L])
        xT, x2T = sb("xT", [P, DC, L]), sb("x2T", [P, DC, L])
        ident = sb("ident", [P, P])
        ones = sb("ones", [P, 1])
        bk_c, bq_c, bv_c = sb("bk_c", [P, DC]), sb("bq_c", [P, DC]), sb("bv_c", [P, DC])
        bo_b = sb("bo_b", [L, D])
        xq, xr, xn, x1, x2n, att = (sb(n, [L, D]) for n in ("xq", "xr", "xn", "x1", "x2n", "att"))
        sq = sb("sq", [L, 2, D])
        cand = sb("cand", [L, G, NCAND])
        top = sb("top", [L, G, TOP])
        topz, csum, gk = (sb(n, [L, G, TOP]) for n in ("topz", "csum", "gk"))
        chain0, inv_k = sb("chain0", [L, G, TOP]), sb("inv_k", [L, G, TOP])
        g_max = sb("g_max", [L, G])
        neg_tau = sb("neg_tau", [L, H])
        row_sum = sb("row_sum", [L, H])
        flag = sb("flag", [L, G + 1])
        flag_i = sb("flag_i", [1, G + 1], I32)
        again = sb("again", [P, 32])
        againT = sb("againT", [P, 32])
        again_m = sb("again_m", [P, 1])
        again_i = sb("again_i", [P, 1], I32)
        count, inv_count, total, delta = (sb(n, [L, 1]) for n in ("count", "inv_count", "total", "delta"))
        eps_t = sb("eps_t", [L, 1])
        eps_c = eps_t[:, :]
        scratch = sb("scratch", [L, N], BF16)
        st1, mv1, sd1 = sb("st1", [L, 6]), sb("mv1", [L, 2]), sb("sd1", [L, 2])
        st2, mv2, sd2 = sb("st2", [L, 6]), sb("mv2", [L, 2]), sb("sd2", [L, 2])

        work = es.enter_context(nc.psum_tensor("work", [P, 2, 2, 512], F32))
        tps = es.enter_context(nc.psum_tensor("tps", [P, 2, 512], F32))
        mix_bank = es.enter_context(nc.psum_tensor("mix_bank", [P, 512], F32))
        flag_bank = es.enter_context(nc.psum_tensor("flag_bank", [P, 512], F32))
        mix_ps, flag_ps = mix_bank[:, 0:L], flag_bank[0:1, 0:G + 1]

        in_ctx, in_xq, in_xr = sem("in_ctx"), sem("in_xq"), sem("in_xr")
        in_wk, in_wq, in_wv, in_wo = sem("in_wk"), sem("in_wq"), sem("in_wv"), sem("in_wo")
        in_bias, in_angle = sem("in_bias"), sem("in_angle")
        stored, store_seen = sem("stored"), sem("store_seen")
        pad_zero, ident0, const_ready, bq_scaled = (sem("pad_zero"), sem("ident0"), sem("const_ready"), sem("bq_scaled"))
        dve_const, angle_step = sem("dve_const"), sem("angle_step")
        angle_ready, ffn_w = sem("angle_ready"), sem("ffn_w")
        work_full = sem("work_full")
        xT_ready, q_raw_ready, qz_ready = (sem(n) for n in ("xT_ready", "q_raw_ready", "qz_ready"))
        ctxT_ready, k_ready, v_ready = sem("ctxT_ready"), sem("k_ready"), sem("v_ready")
        s_ready, tau_ready, relu_done = sem("s_ready"), sem("tau_ready"), sem("relu_done")
        flag_ready, flag_sum, verified = sem("flag_ready"), sem("flag_sum"), sem("verified")
        pT_full, pT_ready, mix_full, mix_read = (sem(n) for n in ("pT_full", "pT_ready", "mix_full", "mix_read"))
        att_ready, x1_ready, res_ready = (sem(n) for n in ("att_ready", "x1_ready", "res_ready"))
        find, tau_step, check_step, fix = sem("find"), sem("tau_step"), sem("check_step"), sem("fix")
        scores_seen = sem("scores_seen")
        ln1_stat, ln1_sd, ln1_step, xn_ready = (sem(n) for n in ("ln1_stat", "ln1_sd", "ln1_step", "xn_ready"))
        ln2_stat, ln2_sd, ln2_step, x2n_ready = (sem(n) for n in ("ln2_stat", "ln2_sd", "ln2_step", "x2n_ready"))
        x2T_ready, sq_ready, sqsum_ready, root_ready, y_ready = (
            sem(n) for n in ("x2T_ready", "sq_ready", "sqsum_ready", "root_ready", "y_ready"))

        block = es.enter_context(nc.Block())

        def passes(eng, one_pass, ring=None):
            one_pass(0, True, False)
            if ring:
                ring.passes = 0
                start = ring.n
            with eng.Fori(1, B - 1) as b:
                if ring:
                    ring.passes = b - 1
                one_pass(b, False, False)
            if ring:
                ring.passes = 0
                assert ring.n - start == ring.per_pass
                ring.n = start + (B - 2) * ring.per_pass
            one_pass(B - 1, False, True)

        @block.sync
        def _(sp):
            def load_ctx(b):
                sp.wait_ge(ctxT_ready, NC // 2 * b)
                src = ctx_in[bass.ds(b, 1), :, :]
                sp.dma_start(ctx_nat[:, 0:NC - 1, :],
                             src[:, 0:(NC - 1) * P, :].rearrange("a (c p) d -> p (a c) d", p=P)).then_inc(in_ctx, 16)
                sp.dma_start(ctx_nat[0:LAST, NC - 1, :],
                             src[:, (NC - 1) * P:N, :].rearrange("a p d -> p (a d)")).then_inc(in_ctx, 16)

            def load_x(buf, b, done):
                sp.dma_start(buf[:, :], x[bass.ds(b, 1), :, :].rearrange("a l d -> l (a d)")).then_inc(done, 16)

            def weight(dst, src, done):
                sp.dma_start(dst, src.rearrange("(c p) n -> p c n", p=P)).then_inc(done, 16)

            load_x(xq, 0, in_xq)
            sp.wait_ge(pad_zero, 1)
            load_ctx(0)
            for dst, src in ((bq_c, bq), (bk_c, bk), (bv_c, bv)):
                sp.dma_start(dst[:, :], src.rearrange("(m p) -> p m", p=P),
                             allow_slow_non_contiguous=True).then_inc(in_bias, 16)
            sp.dma_start(bo_b[:, :], bo.rearrange("(a n) -> a n", a=1).broadcast_to([L, D])).then_inc(in_bias, 16)
            weight(wq[:, :, :], Wq, in_wq)
            weight(wk[:, :, :], Wk, in_wk)
            weight(wcos[:, :, :], theta, in_angle)
            weight(v[:, 0:DC, :], theta_noise, in_angle)
            weight(wsin[:, :, :], phi, in_angle)
            weight(wo[:, :, :], Wo, in_wo)
            weight(wv[:, :, :], Wv, in_wv)
            sp.wait_ge(angle_step, 1)
            weight(v[:, 0:DC, :], phi_noise, in_angle)

            def one_pass(b, first, last):
                if not last:
                    sp.wait_ge(xn_ready, b + 1)
                    load_x(xq, b + 1, in_xq)
                if first:
                    load_x(xr, 0, in_xr)
                else:
                    sp.wait_ge(x1_ready, b)
                    load_x(xr, b, in_xr)
                if not last:
                    load_ctx(b + 1)
                if not first:
                    store(b - 1)
                    sp.wait_ge(stored, 16 * b)
                    sp.sem_inc(store_seen, 1)

            def store(b):
                sp.wait_ge(y_ready, b + 1)
                sp.dma_start(out[bass.ds(b, 1), :, :].rearrange("a l d -> l (a d)"), att[:, :]).then_inc(stored, 16)

            passes(sp, one_pass)
            store(B - 1)
            sp.wait_ge(stored, 16 * B)

        @block.gpsimd
        def _(pool):
            pool.memset(ctx_nat[64:P, NC - 1, :], 0.0).then_inc(pad_zero, 1)
            pool.wait_ge(pad_zero, 1)
            pool.memset(S[:, :, N:NC * P], 0.0).then_inc(pad_zero, 1)
            pool.wait_ge(pad_zero, 2)
            pool.memset(ident[:, :], 0.0).then_inc(ident0, 1)
            pool.wait_ge(ident0, 1)
            pool.affine_select(out=ident[:, :], in_=ident[:, :], compare_op=ALU.not_equal, fill=1.0,
                               base=0, pattern=[[-1, P]], channel_multiplier=1).then_inc(const_ready, 1)
            pool.wait_ge(const_ready, 1)
            pool.memset(ones[:, :], 1.0).then_inc(const_ready, 1)
            pool.wait_ge(const_ready, 2)
            pool.memset(qz[:, :, :, :], 0.0).then_inc(const_ready, 1)
            pool.wait_ge(const_ready, 3)
            pool.wait_ge(in_bias, 64)
            pool.tensor_scalar(bq_c[:, :], bq_c[:, :], SCALE, None, ALU.mult).then_inc(bq_scaled, 1)
            pool.wait_ge(bq_scaled, 1)

            def pad_q(b):
                pool.wait_ge(q_raw_ready, b + 1)
                for j in range(G):
                    r = slice(DH * j, DH * (j + 1))
                    pool.tensor_tensor(qz[r, :, j, :], q_raw[r, :, :],
                                       bq_c[r, :].rearrange("p (m a) -> p m a", a=1).broadcast_to([DH, DC, L]),
                                       ALU.add).then_inc(qz_ready, 1)
                    pool.wait_ge(qz_ready, G * b + j + 1)

            def residual(b):
                pool.wait_ge(in_xr, 16 * (b + 1))
                pool.tensor_tensor(xr[:, :], xr[:, :], bo_b[:, :], ALU.add).then_inc(res_ready, 1)
                pool.wait_ge(res_ready, b + 1)

            pad_q(0)

            def one_pass(b, first, last):
                if not first:
                    pass
                if not last:
                    residual(b)
                    pad_q(b + 1)
                else:
                    residual(b)

            passes(pool, one_pass)

        @block.tensor
        def _(pe):
            ring = Ring(USES)

            def take():
                return work[:, ring.take()[0], :, :]

            def transpose_x(src, psum):
                for c in range(DC):
                    last = nc.tensor.transpose(psum[:, c * L:(c + 1) * L], src[:, c * P:(c + 1) * P], ident[0:L, 0:L])
                return last

            def project(psum, lhs, w):
                for c in range(DC):
                    last = nc.tensor.matmul(psum, lhs(c), w(c), start=(c == 0), stop=(c == DC - 1))
                return last

            def q_of(b):
                pe.wait_ge(xT_ready, b + 1)
                pe.wait_ge(v_ready, NC // 2 * b)
                buf = take()
                for m in range(DC):
                    last = project(buf[:, 0, m * L:(m + 1) * L],
                                   lambda c: wq[:, c, m * P:(m + 1) * P], lambda c: xT[:, c, :])
                last.then_inc(work_full, 1)

            def transpose_ctx(b, x2T_before):
                pe.wait_ge(in_ctx, 32 * (b + 1))
                for i in range(NC // 2):
                    if i == 0:
                        pe.wait_ge(x2T_ready, x2T_before)
                    elif i == 1:
                        pe.wait_ge(q_raw_ready, b + 1)
                    else:
                        pe.wait_ge(ctxT_ready, NC // 2 * b + i - 1)
                    buf = take()
                    for j in range(2):
                        for c in range(DC):
                            last = nc.tensor.transpose(buf[:, j, c * P:(c + 1) * P],
                                                       ctx_nat[:, 2 * i + j, c * P:(c + 1) * P], ident[:, :])
                    last.then_inc(work_full, 1)

            def k_of(b, m, squares_before):
                if m == 0:
                    pe.wait_ge(ctxT_ready, NC // 2 * (b + 1))
                elif m == 1:
                    pe.wait_ge(sq_ready, squares_before)
                else:
                    pe.wait_ge(k_ready, DC * b + m - 1)
                buf = take()
                for half in range(2):
                    last = project(buf[:, half, 0:HALF], lambda c: wk[:, c, m * P:(m + 1) * P],
                                   lambda c: ctxT[:, c, half * HALF:(half + 1) * HALF])
                last.then_inc(work_full, 1)

            def v_of(b, i, first, last_pass):
                if i == 0:
                    pe.wait_ge(s_ready, H * (b + 1))
                elif i == 1:
                    if not first:
                        pe.wait_ge(att_ready, b)
                    if not last_pass:
                        pe.wait_ge(xT_ready, b + 2)
                else:
                    pe.wait_ge(v_ready, NC // 2 * b + i - 1)
                buf = take()
                for j in range(2):
                    kc = 2 * i + j
                    last = project(buf[:, j, :], lambda c: ctxT[:, c, kc * P:(kc + 1) * P], lambda c: wv[:, c, :])
                last.then_inc(work_full, 1)

            def scores(b, h):
                if h == 0:
                    pe.wait_ge(k_ready, DC * (b + 1))
                elif h >= 2:
                    pe.wait_ge(s_ready, H * b + h - 1)
                buf = take()
                for half in range(2):
                    last = nc.tensor.matmul(buf[0:L, half, 0:HALF], qz[:, h // G, h % G, :],
                                            kT[:, h // G, half * HALF:(half + 1) * HALF], start=True, stop=True)
                last.then_inc(work_full, 1)

            def transpose_p(b, g, j):
                if j == 0:
                    pe.wait_ge(verified, DC * b + g + 1)
                h = G * g + j
                for half in range(2):
                    if j > 0:
                        pe.wait_ge(pT_ready, 2 * (H * b + h) + half - 1)
                    for c in range(NC // 2):
                        kc = half * NC // 2 + c
                        last = nc.tensor.transpose(tps[:, half, c * L:(c + 1) * L],
                                                   S[0:L, h, kc * P:(kc + 1) * P], ident[0:L, 0:L])
                    last.then_inc(pT_full, 1)

            def mix(b, g):
                pe.wait_ge(pT_ready, 2 * (H * b + G * (g + 1)))
                if g == 0:
                    pe.wait_ge(v_ready, NC // 2 * (b + 1))
                else:
                    pe.wait_ge(mix_read, DC * b + g)
                for kc in range(NC):
                    for j in range(G):
                        h = G * g + j
                        last = nc.tensor.matmul(mix_ps[DH * j:DH * (j + 1), :], v[:, kc, DH * h:DH * (h + 1)],
                                                pT[:, j, kc * L:(kc + 1) * L],
                                                start=(kc == 0), stop=(kc == NC - 1))
                last.then_inc(mix_full, 1)

            def sum_flags(b, g):
                pe.wait_ge(flag_ready, DC * b + g + 1)
                nc.tensor.matmul(flag_ps, ones[0:L, :], flag[:, :], start=True, stop=True).then_inc(flag_sum, 1)

            def o_of(b, buf):
                pe.wait_ge(mix_read, DC * (b + 1))
                return project(buf[0:L, 0, :], lambda c: aT[:, c, :], lambda c: wo[:, c, :])

            def xT_of(b, buf):
                pe.wait_ge(xn_ready, b + 1)
                return transpose_x(xn, buf[:, 1, :])

            def x2T_of(b, sem_before, value):
                pe.wait_ge(sem_before, value)
                pe.wait_ge(x2n_ready, b + 1)
                transpose_x(x2n, take()[:, 0, :]).then_inc(work_full, 1)

            def ffn_of(b, sem_before, value):
                pe.wait_ge(sem_before, value)
                pe.wait_ge(x2T_ready, b + 1)
                buf = take()
                project(buf[0:L, 0, :], lambda c: x2T[:, c, :], lambda c: wcos[:, c, :])
                project(buf[0:L, 1, :], lambda c: x2T[:, c, :], lambda c: wsin[:, c, :]).then_inc(work_full, 1)

            pe.wait_ge(const_ready, 3)
            xT_of(0, take()).then_inc(work_full, 1)
            pe.wait_ge(in_wq, 16)
            q_of(0)
            transpose_ctx(0, 0)
            pe.wait_ge(in_wk, 16)
            for m in range(DC):
                k_of(0, m, 0)
            pe.wait_ge(in_wo, 16)
            pe.wait_ge(in_wv, 16)

            def one_pass(b, first, last):
                pe.wait_ge(qz_ready, G * (b + 1))
                if not first:
                    for j in range(G):
                        transpose_p(b - 1, 0, j)
                for g in range(DC):
                    if not first:
                        mix(b - 1, g)
                    for j in range(G):
                        scores(b, G * g + j)
                        if not first and g < DC - 1:
                            transpose_p(b - 1, g + 1, j)
                    if g == 0 and not first:
                        sum_flags(b - 1, DC - 1)
                pe.wait_ge(s_ready, H * (b + 1) - 1)
                buf = take()
                if not first:
                    end = o_of(b - 1, buf)
                if not last:
                    end = xT_of(b + 1, buf)
                end.then_inc(work_full, 1)
                v_of(b, 0, first, last)
                sum_flags(b, 0)
                v_of(b, 1, first, last)
                v_of(b, 2, first, last)
                if not first:
                    x2T_of(b - 1, v_ready, NC // 2 * b + 2)
                if not last:
                    q_of(b + 1)
                sum_flags(b, 1)
                if not last:
                    transpose_ctx(b + 1, 0 if first else b)
                if not first:
                    pe.wait_ge(ffn_w, 2)
                    if last:
                        ffn_of(b - 1, v_ready, NC // 2 * (b + 1))
                    else:
                        ffn_of(b - 1, ctxT_ready, NC // 2 * (b + 1) + 2)
                if not last:
                    k_of(b + 1, 0, 0)
                    k_of(b + 1, 1, 0 if first else b)
                sum_flags(b, 2)
                if not last:
                    k_of(b + 1, 2, 0)
                    k_of(b + 1, 3, 0)

            passes(pe, one_pass, ring)
            b = B - 1
            sum_flags(b, DC - 1)
            for g in range(DC):
                for j in range(G):
                    transpose_p(b, g, j)
                mix(b, g)
            pe.wait_ge(x2T_ready, b)
            o_of(b, take()).then_inc(work_full, 1)
            x2T_of(b, sq_ready, b)
            ffn_of(b, att_ready, b + 1)

        @block.scalar
        def _(act):
            ring = Ring(USES)

            def empty():
                slot, n, count_now = ring.take()
                act.wait_ge(work_full, count_now + 1)
                return work[:, slot, :, :]

            def copy(dst, src, **kw):
                return nc.scalar.activation(dst, src, ACT.Copy, **kw)

            def q_of(b):
                copy(q_raw[:, :, :], empty()[:, 0, 0:DC * L].rearrange("p (m l) -> p m l", m=DC),
                     scale=SCALE).then_inc(q_raw_ready, 1)

            def ctxT_of(b, i):
                dst = ctxT[:, :, 2 * i * P:2 * (i + 1) * P].rearrange("p c (j k) -> p j c k", j=2)
                src = empty()
                for j in range(2):
                    last = copy(dst[:, j, :, :], src[:, j, :].rearrange("p (c k) -> p c k", c=DC))
                last.then_inc(ctxT_ready, 1)

            def k_of(b, m):
                nc.scalar.activation(kT[:, m, :].rearrange("p (a n) -> p a n", a=2), empty()[:, :, 0:HALF],
                                     ACT.Identity, bias=bk_c[:, m:m + 1]).then_inc(k_ready, 1)

            def v_of(b, i):
                copy(v[:, 2 * i:2 * i + 2, :], empty()[:, :, :]).then_inc(v_ready, 1)

            def s_of(b, h):
                copy(S[0:L, h, 0:N].rearrange("p (a n) -> p a n", a=2),
                     empty()[0:L, :, 0:HALF]).then_inc(s_ready, 1)

            def relu(b, h):
                if h % G == 0:
                    act.wait_ge(tau_ready, DC * b + h // G + 1)
                nc.scalar.activation(S[0:L, h, 0:N], S[0:L, h, 0:N], ACT.Relu, bias=neg_tau[:, h:h + 1],
                                     accum_out=row_sum[:, h:h + 1]).then_inc(relu_done, 1)

            def pT_of(b, g, j):
                if g > 0:
                    act.wait_ge(mix_full, DC * b + g)
                for half in range(2):
                    act.wait_ge(pT_full, 2 * (H * b + G * g + j) + half + 1)
                    copy(pT[:, j, half * TH:(half + 1) * TH], tps[:, half, 0:TH]).then_inc(pT_ready, 1)

            def mix_of(b, g):
                act.wait_ge(mix_full, DC * b + g + 1)
                nc.scalar.activation(aT[:, g, :], mix_ps, ACT.Identity, bias=bv_c[:, g:g + 1]).then_inc(mix_read, 1)

            def ln_sd(b, mv, sd, stat, done):
                act.wait_ge(stat, b + 1)
                nc.scalar.activation(sd[:, 0:1], mv[:, 1:2], ACT.Sqrt, bias=eps_c).then_inc(done, 1)

            def squares(b):
                nc.scalar.activation(sq[:, :, :], empty()[0:L, :, :], ACT.Square).then_inc(sq_ready, 1)

            def root(b):
                act.wait_ge(sqsum_ready, b + 1)
                nc.scalar.activation(sq[:, 0, :], sq[:, 1, :], ACT.Sqrt).then_inc(root_ready, 1)

            def x2T_of(b):
                copy(x2T[:, :, :], empty()[:, 0, 0:DC * L].rearrange("p (m l) -> p m l", m=DC))\
                    .then_inc(x2T_ready, 1)

            def sines(i, buf):
                act.wait_ge(angle_ready, i + 1)
                nc.scalar.activation(buf[:, :, :], buf[:, :, :], ACT.Sin).then_inc(ffn_w, 1)

            act.wait_ge(dve_const, 3)
            ln_sd(0, mv1, sd1, ln1_stat, ln1_sd)
            copy(xT[:, :, :], empty()[:, 1, 0:DC * L].rearrange("p (m l) -> p m l", m=DC))\
                .then_inc(xT_ready, 1)
            q_of(0)
            for i in range(NC // 2):
                ctxT_of(0, i)
            act.wait_ge(in_bias, 64)
            for m in range(DC):
                k_of(0, m)

            def one_pass(b, first, last):
                if not first:
                    for j in range(G):
                        pT_of(b - 1, 0, j)
                for g in range(DC):
                    if not first:
                        mix_of(b - 1, g)
                    for j in range(G):
                        s_of(b, G * g + j)
                        if not first and g < DC - 1:
                            pT_of(b - 1, g + 1, j)
                        if g == DC - 1:
                            relu(b, j)
                    if g == 1 and not last:
                        ln_sd(b + 1, mv1, sd1, ln1_stat, ln1_sd)
                src = empty()
                if not first:
                    if last:
                        act.wait_ge(stored, 16 * (b - 1))
                    copy(att[:, :], src[0:L, 0, :]).then_inc(att_ready, 1)
                if not last:
                    copy(xT[:, :, :], src[:, 1, 0:DC * L].rearrange("p (m l) -> p m l", m=DC)).then_inc(xT_ready, 1)
                relu(b, G)
                if first:
                    act.wait_ge(angle_step, 9)
                v_of(b, 0)
                relu(b, G + 1)
                v_of(b, 1)
                if first:
                    sines(0, wcos)
                    sines(1, wsin)
                else:
                    ln_sd(b - 1, mv2, sd2, ln2_stat, ln2_sd)
                relu(b, G + 2)
                v_of(b, 2)
                relu(b, G + 3)
                if not first:
                    x2T_of(b - 1)
                relu(b, 2 * G)
                if not last:
                    q_of(b + 1)
                relu(b, 2 * G + 1)
                if not last:
                    ctxT_of(b + 1, 0)
                relu(b, 2 * G + 2)
                if not last:
                    ctxT_of(b + 1, 1)
                relu(b, 2 * G + 3)
                if not last:
                    ctxT_of(b + 1, 2)
                if not first:
                    squares(b - 1)
                for m in range(DC):
                    if not last:
                        k_of(b + 1, m)
                    relu(b, 3 * G + m)
                    if m == 1 and not first:
                        root(b - 1)

            passes(act, one_pass, ring)
            b = B - 1
            for g in range(DC):
                for j in range(G):
                    pT_of(b, g, j)
                mix_of(b, g)
            act.wait_ge(stored, 16 * (B - 1))
            copy(att[:, :], empty()[0:L, 0, :]).then_inc(att_ready, 1)
            ln_sd(b, mv2, sd2, ln2_stat, ln2_sd)
            x2T_of(b)
            squares(b)
            root(b)

        @block.vector
        def _(dve):
            FIND = G + G * (2 * TOP // 8 - 1)

            def layer_norm(b, src, in_wait, stats, mv, sd, dst, stat, sd_done, step, done):
                dve.sem_clear(step)
                in_wait()
                nc.vector.bn_stats(stats[:, :], src[:, :]).then_inc(step, 1)
                dve.wait_ge(step, 1)
                nc.vector.bn_aggr(mv[:, :], stats[:, :]).then_inc(stat, 1)
                dve.wait_ge(sd_done, b + 1)
                nc.vector.reciprocal(sd[:, 1:2], sd[:, 0:1]).then_inc(step, 1)
                dve.wait_ge(step, 2)
                nc.vector.tensor_scalar(dst[:, :], src[:, :], mv[:, 0:1], sd[:, 1:2],
                                        ALU.subtract, ALU.mult).then_inc(done, 1)

            def ln1(b):
                layer_norm(b, xq, lambda: dve.wait_ge(in_xq, 16 * (b + 1)), st1, mv1, sd1, xn,
                           ln1_stat, ln1_sd, ln1_step, xn_ready)

            def thresholds(b, g):
                base = step = 0
                dve.wait_ge(s_ready, H * b + G * (g + 1))
                dve.sem_inc(scores_seen, 1)
                dve.sem_clear(find)
                dve.sem_clear(tau_step)
                for j in range(G):
                    h = G * g + j
                    for i in range(PIECES):
                        last = nc.vector.max(cand[:, j, 8 * i:8 * i + 8], S[0:L, h, cuts[i]:cuts[i + 1]])
                    last.then_inc(find, 1)
                n = G
                for r in range(TOP // 8):
                    for j in range(G):
                        dve.wait_ge(find, base + n - G + j + 1)
                        nc.vector.max(top[:, j, 8 * r:8 * r + 8], cand[:, j, :]).then_inc(find, 1)
                    n += G
                    if r < TOP // 8 - 1:
                        for j in range(G):
                            dve.wait_ge(find, base + n - G + j + 1)
                            nc.vector.match_replace(cand[:, j, :], top[:, j, 8 * r:8 * r + 8], cand[:, j, :],
                                                    LOWEST).then_inc(find, 1)
                        n += G
                assert n == FIND
                dve.wait_ge(find, base + FIND)
                nc.vector.tensor_tensor(topz[:, :, :], top[:, :, :], top[:, :, 0:1].broadcast_to([L, G, TOP]),
                                        ALU.subtract).then_inc(tau_step, 1)
                dve.wait_ge(tau_step, step + 1)
                flat = lambda t: t[:, :, :].rearrange("p g k -> p (g k)")
                nc.vector.tensor_tensor_scan(flat(csum), flat(chain0), flat(topz), 0.0,
                                             ALU.mult, ALU.add).then_inc(tau_step, 1)
                dve.wait_ge(tau_step, step + 2)
                nc.vector.scalar_tensor_tensor(flat(gk), flat(csum), -1.0, flat(inv_k),
                                               ALU.add, ALU.mult).then_inc(tau_step, 1)
                dve.wait_ge(tau_step, step + 3)
                nc.vector.reduce_max(g_max[:, :], gk[:, :, :], AX).then_inc(tau_step, 1)
                dve.wait_ge(tau_step, step + 4)
                nc.vector.scalar_tensor_tensor(neg_tau[:, G * g:G * (g + 1)], g_max[:, :], -1.0, top[:, :, 0],
                                               ALU.mult, ALU.subtract).then_inc(tau_ready, 1)

            def newton(h, n):
                p = S[0:L, h, 0:N]
                nc.vector.tensor_scalar(scratch[:, :], p, 0.0, None, ALU.is_gt, ALU.add,
                                        accum_out=count[:, :]).then_inc(fix, 1)
                dve.wait_ge(fix, n + 1)
                nc.vector.tensor_scalar(scratch[:, :], p, 1.0, None, ALU.mult, ALU.add,
                                        accum_out=total[:, :]).then_inc(fix, 1)
                nc.vector.reciprocal(inv_count[:, :], count[:, :]).then_inc(fix, 1)
                dve.wait_ge(fix, n + 3)
                nc.vector.scalar_tensor_tensor(delta[:, :], total[:, :], -1.0, inv_count[:, :],
                                               ALU.add, ALU.mult).then_inc(fix, 1)
                dve.wait_ge(fix, n + 4)
                nc.vector.tensor_scalar(delta[:, :], delta[:, :], 0.0, None, ALU.max).then_inc(fix, 1)
                dve.wait_ge(fix, n + 5)
                nc.vector.tensor_scalar(p, p, delta[:, :], 0.0, ALU.subtract, ALU.max).then_inc(fix, 1)
                dve.wait_ge(fix, n + 6)
                return n + 6

            def refine(h):
                dve.sem_clear(fix)
                n = newton(h, 0)
                n = newton(h, n)
                nc.vector.tensor_scalar(scratch[:, :], S[0:L, h, 0:N], 1.0, None, ALU.mult, ALU.add,
                                        accum_out=total[:, :]).then_inc(fix, 1)
                dve.wait_ge(fix, n + 1)
                nc.vector.tensor_scalar(again[0:L, 0:1], total[:, :], 1.0 + SUM_TOL, None, ALU.is_gt).then_inc(fix, 1)
                dve.wait_ge(fix, n + 2)
                nc.vector.transpose(againT[:, :], again[:, :]).then_inc(fix, 1)
                dve.wait_ge(fix, n + 3)
                nc.vector.reduce_max(again_m[:, :], againT[:, :], AX).then_inc(fix, 1)
                dve.wait_ge(fix, n + 4)
                nc.vector.tensor_copy(again_i[:, :], again_m[:, :]).then_inc(fix, 1)
                dve.wait_ge(fix, n + 5)
                left = [dve.value_load(again_i[32 * q:32 * q + 1, 0:1], min_val=0, max_val=1) for q in range(P // 32)]
                with dve.If(left[0] + left[1] + left[2] + left[3] > 0):
                    with dve.Fori(0, NEWTON_MAX) as _:
                        dve.sem_clear(fix)
                        newton(h, 0)

            def mark(b, g):
                dve.wait_ge(relu_done, H * b + G * (g + 1))
                nc.vector.tensor_scalar(flag[:, 0:G], row_sum[:, G * g:G * (g + 1)], 1.0 + SUM_TOL, None,
                                        ALU.is_gt, ALU.add, accum_out=flag[:, G:G + 1]).then_inc(flag_ready, 1)

            def settle(b, g):
                dve.sem_clear(check_step)
                dve.wait_ge(flag_sum, DC * b + g + 1)
                nc.vector.tensor_copy(flag_i[:, :], flag_ps).then_inc(check_step, 1)
                dve.wait_ge(check_step, 1)
                with dve.If(dve.value_load(flag_i[0:1, G:G + 1], min_val=0, max_val=G * L) > 0):
                    for j in range(G):
                        with dve.If(dve.value_load(flag_i[0:1, j:j + 1], min_val=0, max_val=L) > 0):
                            refine(G * g + j)
                dve.sem_inc(verified, 1)

            def tail1(b):
                def x1_of():
                    dve.wait_ge(att_ready, b + 1)
                    dve.wait_ge(res_ready, b + 1)
                    nc.vector.tensor_tensor(x1[:, :], att[:, :], xr[:, :], ALU.add).then_inc(x1_ready, 1)
                    dve.wait_ge(x1_ready, b + 1)
                layer_norm(b, x1, x1_of, st2, mv2, sd2, x2n, ln2_stat, ln2_sd, ln2_step, x2n_ready)

            def tail2(b):
                dve.wait_ge(sq_ready, b + 1)
                nc.vector.tensor_tensor(sq[:, 1, :], sq[:, 0, :], sq[:, 1, :], ALU.add).then_inc(sqsum_ready, 1)
                dve.wait_ge(root_ready, b + 1)
                nc.vector.tensor_tensor(att[:, :], x1[:, :], sq[:, 0, :], ALU.add).then_inc(y_ready, 1)

            def angles(i, w, shift):
                n = [4 * i]
                turns = pT[:, :, :].rearrange("p g n -> p (g n)")[:, 0:DC * D].rearrange("p (c n) -> p c n", c=DC)

                def link(ins):
                    ins.then_inc(angle_step, 1)
                    n[0] += 1
                    dve.wait_ge(angle_step, n[0])

                n[0] = 8 * i
                link(nc.vector.tensor_tensor(w[:, :, :], w[:, :, :], v[:, 0:DC, :], ALU.add))
                link(nc.vector.tensor_scalar(turns, w[:, :, :], shift, 1.0 / TWO_PI, ALU.add, ALU.mult))
                link(nc.vector.tensor_scalar(turns, turns, ROUND, None, ALU.add))
                link(nc.vector.tensor_scalar(turns, turns, ROUND, None, ALU.subtract))
                link(nc.vector.scalar_tensor_tensor(w[:, :, :], turns, -TWO_PI_HI, w[:, :, :], ALU.mult, ALU.add))
                link(nc.vector.scalar_tensor_tensor(w[:, :, :], turns, -TWO_PI_LO, w[:, :, :], ALU.mult, ALU.add))
                link(nc.vector.tensor_scalar(w[:, :, :], w[:, :, :], shift, PI_BELOW, ALU.add, ALU.min))
                link(nc.vector.tensor_scalar(w[:, :, :], w[:, :, :], -PI_BELOW, None, ALU.max))
                dve.sem_inc(angle_ready, 1)

            nc.vector.memset(chain0[:, :, 1:TOP], 1.0)
            nc.vector.memset(chain0[:, :, 0:1], 0.0)
            nc.vector.memset(again[:, :], 0.0)
            for k in range(TOP):
                last = nc.vector.memset(inv_k[:, :, k:k + 1], 1.0 / (k + 1))
            last.then_inc(dve_const, 1)
            nc.vector.memset(eps_c, LN_EPS).then_inc(dve_const, 2)
            dve.wait_ge(dve_const, 3)
            ln1(0)
            dve.wait_ge(in_angle, 48)
            angles(0, wcos, TWO_PI / 4)
            dve.wait_ge(in_angle, 64)
            angles(1, wsin, 0.0)

            def one_pass(b, first, last):
                if not first:
                    mark(b - 1, 3)
                thresholds(b, 0)
                if not first:
                    settle(b - 1, 3)
                if not last:
                    ln1(b + 1)
                thresholds(b, 1)
                mark(b, 0)
                thresholds(b, 2)
                settle(b, 0)
                if not first:
                    tail1(b - 1)
                mark(b, 1)
                thresholds(b, 3)
                settle(b, 1)
                mark(b, 2)
                if not first:
                    tail2(b - 1)
                settle(b, 2)

            passes(dve, one_pass)
            mark(B - 1, 3)
            settle(B - 1, 3)
            tail1(B - 1)
            tail2(B - 1)


_INS = ["x", "ctx_1024", "L0_xattn_Wq", "L0_xattn_bq", "L0_xattn_Wk", "L0_xattn_bk", "L0_xattn_Wv", "L0_xattn_bv",
        "L0_xattn_Wo", "L0_xattn_bo", "L0_ffn_theta", "L0_ffn_phi", "L0_ffn_theta_noise", "L0_ffn_phi_noise"]


def kernel(**inputs):
    import numpy as np
    import concourse.bacc as bacc
    from concourse.bass_utils import run_bass_kernel_spmd

    nc = bacc.Bacc("TRN2", target_bir_lowering=False, num_devices=1)
    arrays, args = {}, []
    for name in _INS:
        a = np.ascontiguousarray(inputs[name])
        arrays[f"in_{name}"] = a
        args.append(nc.dram_tensor(f"in_{name}", a.shape, mybir.dt.from_np(a.dtype), kind="ExternalInput").ap())
    args.append(nc.dram_tensor("out_y", inputs["x"].shape, F32, kind="ExternalOutput").ap())
    build_kernel(nc, *args)
    r = run_bass_kernel_spmd(nc, [arrays], core_ids=[0])
    return r.results[0]["out_y"]
```

```python
from contextlib import ExitStack

import concourse.bass as bass
from concourse import mybir

F32 = mybir.dt.float32
BF16 = mybir.dt.bfloat16
F16 = mybir.dt.float16
I32 = mybir.dt.int32
ALU = mybir.AluOpType
ACT = mybir.ActivationFunctionType
AX = mybir.AxisListType.X

P = 128
TWO_PI = 6.283185307179586
TWO_PI_HI = 6.28125
TWO_PI_LO = TWO_PI - TWO_PI_HI
ROUND = 1.5 * 2.0 ** 23
PI_BELOW = 3.1415925
W_SCALE = 64.0
LN_EPS = 1e-5
SUM_TOL = 1e-5
TOP = 40
PIECES = 12
NEWTON_MAX = 28
LOWEST = -3.0e38


class Ring:

    def __init__(self, per_pass):
        self.n, self.per_pass, self.passes = 0, per_pass, 0

    def take(self):
        n = self.n
        self.n += 1
        return n % 2, n, n + self.passes * self.per_pass if self.per_pass else n


def build_kernel(nc, x, ctx_in, Wq, bq, Wk, bk, Wv, bv, Wo, bo, theta, phi, theta_noise, phi_noise, out):
    B, L, D = x.shape
    N = ctx_in.shape[1]
    H = 16
    DH = D // H
    DC = D // P
    G = H // DC
    NC = -(-N // P)
    LAST = N - (NC - 1) * P
    HALF = N // 2
    TH = NC // 2 * L
    SCALE = float(DH) ** -0.5
    NCAND = 8 * PIECES
    cuts = [N * i // PIECES for i in range(PIECES + 1)]
    USES = H + 1 + NC // 2 + 1 + 1 + NC // 2 + 1 + DC

    assert D == DC * P and H == DC * G and N == 2 * HALF and NC % 2 == 0 and USES % 2 == 0

    es = ExitStack()
    with es:
        def sb(name, shape, dt=F32):
            return es.enter_context(nc.sbuf_tensor(name, shape, dt))

        def sem(name):
            return es.enter_context(nc.semaphore(name))

        wq, wo = sb("wq", [P, DC, D]), sb("wo", [P, DC, D])
        wk2, wv2 = sb("wk2", [P, 2, DC, D], F16), sb("wv2", [P, 2, DC, D], F16)
        wcos, wsin = sb("wcos", [P, DC, D]), sb("wsin", [P, DC, D])
        ctx_nat = sb("ctx_nat", [P, NC, D])
        ctxT2 = sb("ctxT2", [P, 2, DC, NC * P], F16)
        ctxT_f = sb("ctxT_f", [P, DC, 2 * P])
        kT2 = sb("kT2", [P, 2, DC, N], F16)
        k_f = sb("k_f", [P, 2, N])
        v = sb("v", [P, NC, D])
        S = sb("S", [P, H, NC * P])
        pT = sb("pT", [P, G, NC * L])
        qz2 = sb("qz2", [P, 2, DC, G, L], F16)
        q_raw = sb("q_raw", [P, DC, L])
        aT = sb("aT", [P, DC, L])
        xT, x2T = sb("xT", [P, DC, L]), sb("x2T", [P, DC, L])
        ident = sb("ident", [P, P])
        ones = sb("ones", [P, 1])
        bk_c, bq_c, bv_c = sb("bk_c", [P, DC]), sb("bq_c", [P, DC]), sb("bv_c", [P, DC])
        bo_b = sb("bo_b", [L, D])
        xq, xr, xn, x1, x2n, att = (sb(n, [L, D]) for n in ("xq", "xr", "xn", "x1", "x2n", "att"))
        sq = sb("sq", [L, 2, D])
        cand = sb("cand", [L, G, NCAND])
        top = sb("top", [L, G, TOP])
        topz, csum, gk = (sb(n, [L, G, TOP]) for n in ("topz", "csum", "gk"))
        chain0, inv_k = sb("chain0", [L, G, TOP]), sb("inv_k", [L, G, TOP])
        g_max = sb("g_max", [L, G])
        neg_tau = sb("neg_tau", [L, H])
        row_sum = sb("row_sum", [L, H])
        flag = sb("flag", [L, G + 1])
        flag_i = sb("flag_i", [1, G + 1], I32)
        again = sb("again", [P, 32])
        againT = sb("againT", [P, 32])
        again_m = sb("again_m", [P, 1])
        again_i = sb("again_i", [P, 1], I32)
        count, inv_count, total, delta = (sb(n, [L, 1]) for n in ("count", "inv_count", "total", "delta"))
        eps_t = sb("eps_t", [L, 1])
        eps_c = eps_t[:, :]
        scratch = cand[:, :, :].rearrange("p g n -> p (g n)").bitcast(BF16)[:, 0:N]
        st1, mv1, sd1 = sb("st1", [L, 6]), sb("mv1", [L, 2]), sb("sd1", [L, 2])
        st2, mv2, sd2 = sb("st2", [L, 6]), sb("mv2", [L, 2]), sb("sd2", [L, 2])

        work = es.enter_context(nc.psum_tensor("work", [P, 2, 2, 512], F32))
        tps = es.enter_context(nc.psum_tensor("tps", [P, 2, 512], F32))
        mix_bank = es.enter_context(nc.psum_tensor("mix_bank", [P, 512], F32))
        flag_bank = es.enter_context(nc.psum_tensor("flag_bank", [P, 512], F32))
        mix_ps, flag_ps = mix_bank[:, 0:L], flag_bank[0:1, 0:G + 1]

        in_ctx, in_xq, in_xr = sem("in_ctx"), sem("in_xq"), sem("in_xr")
        in_wk, in_wq, in_wv, in_wo = sem("in_wk"), sem("in_wq"), sem("in_wv"), sem("in_wo")
        in_bias, in_angle = sem("in_bias"), sem("in_angle")
        stored, store_seen = sem("stored"), sem("store_seen")
        pad_zero, ident0, const_ready, bq_scaled = (sem("pad_zero"), sem("ident0"), sem("const_ready"), sem("bq_scaled"))
        dve_const, angle_step = sem("dve_const"), sem("angle_step")
        angle_ready, ffn_w = sem("angle_ready"), sem("ffn_w")
        work_full = sem("work_full")
        weight_step, split_ready = sem("weight_step"), sem("split_ready")
        ctx_f_ready, k_f_ready, q_sum = sem("ctx_f_ready"), sem("k_f_ready"), sem("q_sum")
        ctx_lo_ready, k_lo_ready = sem("ctx_lo_ready"), sem("k_lo_ready")
        xT_ready, q_raw_ready, qz_ready = (sem(n) for n in ("xT_ready", "q_raw_ready", "qz_ready"))
        v_ready = sem("v_ready")
        s_ready, tau_ready, relu_done = sem("s_ready"), sem("tau_ready"), sem("relu_done")
        flag_ready, flag_sum, verified = sem("flag_ready"), sem("flag_sum"), sem("verified")
        pT_full, pT_ready, mix_full, mix_read = (sem(n) for n in ("pT_full", "pT_ready", "mix_full", "mix_read"))
        att_ready, x1_ready, res_ready = (sem(n) for n in ("att_ready", "x1_ready", "res_ready"))
        find, tau_step, check_step, fix = sem("find"), sem("tau_step"), sem("check_step"), sem("fix")
        scores_seen = sem("scores_seen")
        ln1_stat, ln1_sd, ln1_step, xn_ready = (sem(n) for n in ("ln1_stat", "ln1_sd", "ln1_step", "xn_ready"))
        ln2_stat, ln2_sd, ln2_step, x2n_ready = (sem(n) for n in ("ln2_stat", "ln2_sd", "ln2_step", "x2n_ready"))
        x2T_ready, sq_ready, sqsum_ready, root_ready, y_ready = (
            sem(n) for n in ("x2T_ready", "sq_ready", "sqsum_ready", "root_ready", "y_ready"))

        block = es.enter_context(nc.Block())

        def passes(eng, one_pass, ring=None):
            one_pass(0, True, False)
            if ring:
                ring.passes = 0
                start = ring.n
            with eng.Fori(1, B - 1) as b:
                if ring:
                    ring.passes = b - 1
                one_pass(b, False, False)
            if ring:
                ring.passes = 0
                assert ring.n - start == ring.per_pass
                ring.n = start + (B - 2) * ring.per_pass
            one_pass(B - 1, False, True)

        @block.sync
        def _(sp):
            def load_ctx(b):
                sp.wait_ge(ctx_f_ready, NC // 2 * b)
                src = ctx_in[bass.ds(b, 1), :, :]
                sp.dma_start(ctx_nat[:, 0:NC - 1, :],
                             src[:, 0:(NC - 1) * P, :].rearrange("a (c p) d -> p (a c) d", p=P)).then_inc(in_ctx, 16)
                sp.dma_start(ctx_nat[0:LAST, NC - 1, :],
                             src[:, (NC - 1) * P:N, :].rearrange("a p d -> p (a d)")).then_inc(in_ctx, 16)

            def load_x(buf, b, done):
                sp.dma_start(buf[:, :], x[bass.ds(b, 1), :, :].rearrange("a l d -> l (a d)")).then_inc(done, 16)

            def weight(dst, src, done):
                sp.dma_start(dst, src.rearrange("(c p) n -> p c n", p=P)).then_inc(done, 16)

            load_x(xq, 0, in_xq)
            sp.wait_ge(pad_zero, 1)
            load_ctx(0)
            for dst, src in ((bq_c, bq), (bk_c, bk), (bv_c, bv)):
                sp.dma_start(dst[:, :], src.rearrange("(m p) -> p m", p=P),
                             allow_slow_non_contiguous=True).then_inc(in_bias, 16)
            sp.dma_start(bo_b[:, :], bo.rearrange("(a n) -> a n", a=1).broadcast_to([L, D])).then_inc(in_bias, 16)
            weight(wq[:, :, :], Wq, in_wq)
            weight(S[:, 0:DC, 0:D], Wk, in_wk)
            weight(S[:, DC:2 * DC, 0:D], Wv, in_wv)
            weight(wcos[:, :, :], theta, in_angle)
            weight(v[:, 0:DC, :], theta_noise, in_angle)
            weight(wsin[:, :, :], phi, in_angle)
            weight(wo[:, :, :], Wo, in_wo)
            sp.wait_ge(angle_step, 1)
            weight(v[:, 0:DC, :], phi_noise, in_angle)

            def one_pass(b, first, last):
                if not last:
                    sp.wait_ge(xn_ready, b + 1)
                    load_x(xq, b + 1, in_xq)
                    load_ctx(b + 1)
                if first:
                    load_x(xr, 0, in_xr)
                else:
                    sp.wait_ge(x1_ready, b)
                    load_x(xr, b, in_xr)
                if not first:
                    store(b - 1)
                    sp.wait_ge(stored, 16 * b)
                    sp.sem_inc(store_seen, 1)

            def store(b):
                sp.wait_ge(y_ready, b + 1)
                sp.dma_start(out[bass.ds(b, 1), :, :].rearrange("a l d -> l (a d)"), att[:, :]).then_inc(stored, 16)

            passes(sp, one_pass)
            store(B - 1)
            sp.wait_ge(stored, 16 * B)

        @block.gpsimd
        def _(pool):
            pool.memset(ctx_nat[64:P, NC - 1, :], 0.0).then_inc(pad_zero, 1)
            pool.wait_ge(pad_zero, 1)
            pool.memset(S[:, :, N:NC * P], 0.0).then_inc(pad_zero, 1)
            pool.wait_ge(pad_zero, 2)
            pool.memset(ident[:, :], 0.0).then_inc(ident0, 1)
            pool.wait_ge(ident0, 1)
            pool.affine_select(out=ident[:, :], in_=ident[:, :], compare_op=ALU.not_equal, fill=1.0,
                               base=0, pattern=[[-1, P]], channel_multiplier=1).then_inc(const_ready, 1)
            pool.wait_ge(const_ready, 1)
            pool.memset(ones[:, :], 1.0).then_inc(const_ready, 1)
            pool.wait_ge(const_ready, 2)
            pool.memset(qz2[:, :, :, :, :], 0.0).then_inc(const_ready, 1)
            pool.wait_ge(const_ready, 3)
            pool.wait_ge(in_bias, 64)
            pool.tensor_scalar(bq_c[:, :], bq_c[:, :], SCALE, None, ALU.mult).then_inc(bq_scaled, 1)
            pool.wait_ge(bq_scaled, 1)

            def pad_q(b):
                pool.wait_ge(q_raw_ready, b + 1)
                for j in range(G):
                    r = slice(DH * j, DH * (j + 1))
                    pool.tensor_tensor(qz2[r, 0, :, j, :], q_raw[r, :, :],
                                       bq_c[r, :].rearrange("p (m a) -> p m a", a=1).broadcast_to([DH, DC, L]),
                                       ALU.add).then_inc(qz_ready, 1)
                    pool.wait_ge(qz_ready, 2 * G * b + j + 1)
                pool.tensor_tensor(q_raw[:, :, :], q_raw[:, :, :],
                                   bq_c[:, :].rearrange("p (m a) -> p m a", a=1).broadcast_to([P, DC, L]),
                                   ALU.add).then_inc(q_sum, 1)
                pool.wait_ge(q_sum, b + 1)
                for j in range(G):
                    r = slice(DH * j, DH * (j + 1))
                    pool.tensor_tensor(qz2[r, 1, :, j, :], q_raw[r, :, :], qz2[r, 0, :, j, :],
                                       ALU.subtract).then_inc(qz_ready, 1)
                    pool.wait_ge(qz_ready, 2 * G * b + G + j + 1)

            def low_ctx(b, i):
                pool.wait_ge(ctx_f_ready, NC // 2 * b + i + 1)
                at = slice(2 * i * P, 2 * (i + 1) * P)
                pool.tensor_tensor(ctxT2[:, 1, :, at], ctxT_f[:, :, :], ctxT2[:, 0, :, at],
                                   ALU.subtract).then_inc(ctx_lo_ready, 1)
                pool.wait_ge(ctx_lo_ready, NC // 2 * b + i + 1)

            def low_k(b, m):
                pool.wait_ge(k_f_ready, DC * b + m + 1)
                pool.tensor_tensor(kT2[:, 1, m, :], k_f[:, m % 2, :], kT2[:, 0, m, :],
                                   ALU.subtract).then_inc(k_lo_ready, 1)
                pool.wait_ge(k_lo_ready, DC * b + m + 1)

            def prepare(b):
                for i in range(NC // 2):
                    low_ctx(b, i)
                pad_q(b)
                for m in range(DC):
                    low_k(b, m)

            def residual(b):
                pool.wait_ge(in_xr, 16 * (b + 1))
                pool.tensor_tensor(xr[:, :], xr[:, :], bo_b[:, :], ALU.add).then_inc(res_ready, 1)
                pool.wait_ge(res_ready, b + 1)

            prepare(0)

            def one_pass(b, first, last):
                if not last:
                    prepare(b + 1)
                residual(b)

            passes(pool, one_pass)

        @block.tensor
        def _(pe):
            ring = Ring(USES)

            def take():
                return work[:, ring.take()[0], :, :]

            def transpose_x(src, psum):
                for c in range(DC):
                    last = nc.tensor.transpose(psum[:, c * L:(c + 1) * L], src[:, c * P:(c + 1) * P], ident[0:L, 0:L])
                return last

            def project2(psum, lhs, w):
                terms = [(c, i, j) for c in range(DC) for i, j in ((0, 0), (0, 1), (1, 0))]
                for n, (c, i, j) in enumerate(terms):
                    last = nc.tensor.matmul(psum, lhs(c, i), w(c, j), start=(n == 0), stop=(n == len(terms) - 1))
                return last

            def project(psum, lhs, w):
                for c in range(DC):
                    last = nc.tensor.matmul(psum, lhs(c), w(c), start=(c == 0), stop=(c == DC - 1))
                return last

            def q_of(b):
                pe.wait_ge(xT_ready, b + 1)
                pe.wait_ge(ctx_f_ready, NC // 2 * (b + 1))
                buf = take()
                for m in range(DC):
                    last = project(buf[:, 0, m * L:(m + 1) * L],
                                   lambda c: wq[:, c, m * P:(m + 1) * P], lambda c: xT[:, c, :])
                last.then_inc(work_full, 1)

            def transpose_ctx(b, i, att_before=0):
                if i > 0:
                    pe.wait_ge(ctx_f_ready, NC // 2 * b + i)
                else:
                    pe.wait_ge(in_ctx, 32 * (b + 1))
                    pe.wait_ge(xT_ready, b + 1)
                    if att_before is not None:
                        pe.wait_ge(att_ready, att_before)
                buf = take()
                for j in range(2):
                    for c in range(DC):
                        last = nc.tensor.transpose(buf[:, j, c * P:(c + 1) * P],
                                                   ctx_nat[:, 2 * i + j, c * P:(c + 1) * P], ident[:, :])
                last.then_inc(work_full, 1)

            def k_of(b, m, squares_before):
                if m == 0:
                    pe.wait_ge(ctx_lo_ready, NC // 2 * (b + 1))
                    pe.wait_ge(q_raw_ready, b + 1)
                elif m == 1:
                    pe.wait_ge(sq_ready, squares_before)
                else:
                    pe.wait_ge(k_f_ready, DC * b + m - 1)
                buf = take()
                for half in range(2):
                    last = project2(buf[:, half, 0:HALF], lambda c, i: wk2[:, i, c, m * P:(m + 1) * P],
                                    lambda c, j: ctxT2[:, j, c, half * HALF:(half + 1) * HALF])
                last.then_inc(work_full, 1)

            def v_of(b, i, last_pass):
                if i == 0:
                    pe.wait_ge(s_ready, H * (b + 1))
                else:
                    pe.wait_ge(v_ready, NC // 2 * b + i)
                    if last_pass:
                        pe.wait_ge(att_ready, b)
                buf = take()
                for j in range(2):
                    kc = 2 * i + j
                    last = project2(buf[:, j, :], lambda c, i: ctxT2[:, i, c, kc * P:(kc + 1) * P],
                                    lambda c, j: wv2[:, j, c, :])
                last.then_inc(work_full, 1)

            def scores(b, h):
                if h == 0:
                    pe.wait_ge(k_lo_ready, DC * (b + 1))
                elif h >= 2:
                    pe.wait_ge(s_ready, H * b + h - 1)
                buf = take()
                for half in range(2):
                    for n, (i, j) in enumerate(((0, 0), (0, 1), (1, 0))):
                        last = nc.tensor.matmul(buf[0:L, half, 0:HALF], qz2[:, i, h // G, h % G, :],
                                                kT2[:, j, h // G, half * HALF:(half + 1) * HALF],
                                                start=(n == 0), stop=(n == 2))
                last.then_inc(work_full, 1)

            def transpose_p(b, g, j):
                if j == 0:
                    pe.wait_ge(verified, DC * b + g + 1)
                h = G * g + j
                for half in range(2):
                    if j > 0:
                        pe.wait_ge(pT_ready, 2 * (H * b + h) + half - 1)
                    for c in range(NC // 2):
                        kc = half * NC // 2 + c
                        last = nc.tensor.transpose(tps[:, half, c * L:(c + 1) * L],
                                                   S[0:L, h, kc * P:(kc + 1) * P], ident[0:L, 0:L])
                    last.then_inc(pT_full, 1)

            def mix(b, g):
                pe.wait_ge(pT_ready, 2 * (H * b + G * (g + 1)))
                if g == 0:
                    pe.wait_ge(v_ready, NC // 2 * (b + 1))
                else:
                    pe.wait_ge(mix_read, DC * b + g)
                for kc in range(NC):
                    for j in range(G):
                        h = G * g + j
                        last = nc.tensor.matmul(mix_ps[DH * j:DH * (j + 1), :], v[:, kc, DH * h:DH * (h + 1)],
                                                pT[:, j, kc * L:(kc + 1) * L],
                                                start=(kc == 0), stop=(kc == NC - 1))
                last.then_inc(mix_full, 1)

            def sum_flags(b, g):
                pe.wait_ge(flag_ready, DC * b + g + 1)
                nc.tensor.matmul(flag_ps, ones[0:L, :], flag[:, :], start=True, stop=True).then_inc(flag_sum, 1)

            def o_of(b, buf):
                pe.wait_ge(mix_read, DC * (b + 1))
                return project(buf[0:L, 0, :], lambda c: aT[:, c, :], lambda c: wo[:, c, :])

            def xT_of(b, buf):
                pe.wait_ge(xn_ready, b + 1)
                return transpose_x(xn, buf[:, 1, :])

            def x2T_of(b, sem_before, value):
                pe.wait_ge(sem_before, value)
                pe.wait_ge(x2n_ready, b + 1)
                transpose_x(x2n, take()[:, 0, :]).then_inc(work_full, 1)

            def ffn_of(b, sem_before, value):
                pe.wait_ge(sem_before, value)
                pe.wait_ge(x2T_ready, b + 1)
                buf = take()
                project(buf[0:L, 0, :], lambda c: x2T[:, c, :], lambda c: wcos[:, c, :])
                project(buf[0:L, 1, :], lambda c: x2T[:, c, :], lambda c: wsin[:, c, :]).then_inc(work_full, 1)

            pe.wait_ge(const_ready, 3)
            xT_of(0, take()).then_inc(work_full, 1)
            for i in range(NC // 2):
                transpose_ctx(0, i, None)
            pe.wait_ge(in_wq, 16)
            q_of(0)
            pe.wait_ge(split_ready, 1)
            for m in range(DC):
                k_of(0, m, 0)
            pe.wait_ge(in_wo, 16)
            pe.wait_ge(split_ready, 2)

            def one_pass(b, first, last):
                pe.wait_ge(qz_ready, 2 * G * (b + 1))
                for g in range(DC):
                    for j in range(G):
                        if not first and g < DC - 1:
                            transpose_p(b - 1, g + 1, j)
                        scores(b, G * g + j)
                        if g == 0 and j == 1 and not first:
                            sum_flags(b - 1, DC - 1)
                    if not first and g < DC - 1:
                        mix(b - 1, g + 1)
                pe.wait_ge(s_ready, H * (b + 1) - 1)
                buf = take()
                if not first:
                    end = o_of(b - 1, buf)
                if not last:
                    end = xT_of(b + 1, buf)
                end.then_inc(work_full, 1)
                for i in range(NC // 2):
                    v_of(b, i, last)
                    if not last:
                        transpose_ctx(b + 1, i, None if first else b)
                    if i == 0:
                        sum_flags(b, 0)
                if not first:
                    x2T_of(b - 1, v_ready, NC // 2 * (b + 1))
                if not last:
                    q_of(b + 1)
                sum_flags(b, 1)
                if not first:
                    pe.wait_ge(ffn_w, 2)
                    ffn_of(b - 1, v_ready, NC // 2 * (b + 1))
                for m in range(DC):
                    transpose_p(b, 0, m)
                    if not last:
                        k_of(b + 1, m, 0 if first else b)
                    if m == 2:
                        sum_flags(b, 2)
                mix(b, 0)

            passes(pe, one_pass, ring)
            b = B - 1
            sum_flags(b, DC - 1)
            for g in range(1, DC):
                for j in range(G):
                    transpose_p(b, g, j)
                mix(b, g)
            pe.wait_ge(x2T_ready, b)
            o_of(b, take()).then_inc(work_full, 1)
            x2T_of(b, sq_ready, b)
            ffn_of(b, att_ready, b + 1)

        @block.scalar
        def _(act):
            ring = Ring(USES)

            def empty():
                slot, n, count_now = ring.take()
                act.wait_ge(work_full, count_now + 1)
                return work[:, slot, :, :]

            def at_start(b):
                return isinstance(b, int) and b == 0

            def copy(dst, src, **kw):
                return nc.scalar.activation(dst, src, ACT.Copy, **kw)

            def q_of(b):
                copy(q_raw[:, :, :], empty()[:, 0, 0:DC * L].rearrange("p (m l) -> p m l", m=DC),
                     scale=SCALE).then_inc(q_raw_ready, 1)

            def ctxT_of(b, i):
                src = empty()
                if i > 0 or not at_start(b):
                    act.wait_ge(ctx_lo_ready, NC // 2 * b + i)
                for part, dst in ((0, ctxT2[:, 0, :, 2 * i * P:2 * (i + 1) * P]), (1, ctxT_f[:, :, :])):
                    for j in range(2):
                        last = copy(dst[:, :, j * P:(j + 1) * P], src[:, j, :].rearrange("p (c k) -> p c k", c=DC))
                last.then_inc(ctx_f_ready, 1)

            def k_of(b, m):
                src = empty()
                if m > 1 or not at_start(b):
                    act.wait_ge(k_lo_ready, DC * b + m - 1)
                for dst in (kT2[:, 0, m, :], k_f[:, m % 2, :]):
                    last = nc.scalar.activation(dst.rearrange("p (a n) -> p a n", a=2), src[:, :, 0:HALF],
                                                ACT.Identity, bias=bk_c[:, m:m + 1], scale=1.0 / W_SCALE)
                last.then_inc(k_f_ready, 1)

            def v_of(b, i):
                copy(v[:, 2 * i:2 * i + 2, :], empty()[:, :, :], scale=1.0 / W_SCALE).then_inc(v_ready, 1)

            def s_of(b, h):
                copy(S[0:L, h, 0:N].rearrange("p (a n) -> p a n", a=2),
                     empty()[0:L, :, 0:HALF]).then_inc(s_ready, 1)

            def relu(b, h):
                if h % G == 0:
                    act.wait_ge(tau_ready, DC * b + h // G + 1)
                nc.scalar.activation(S[0:L, h, 0:N], S[0:L, h, 0:N], ACT.Relu, bias=neg_tau[:, h:h + 1],
                                     accum_out=row_sum[:, h:h + 1]).then_inc(relu_done, 1)

            def pT_of(b, g, j):
                if g > 0:
                    act.wait_ge(mix_full, DC * b + g)
                for half in range(2):
                    act.wait_ge(pT_full, 2 * (H * b + G * g + j) + half + 1)
                    copy(pT[:, j, half * TH:(half + 1) * TH], tps[:, half, 0:TH]).then_inc(pT_ready, 1)

            def mix_of(b, g):
                act.wait_ge(mix_full, DC * b + g + 1)
                nc.scalar.activation(aT[:, g, :], mix_ps, ACT.Identity, bias=bv_c[:, g:g + 1]).then_inc(mix_read, 1)

            def ln_sd(b, mv, sd, stat, done):
                act.wait_ge(stat, b + 1)
                nc.scalar.activation(sd[:, 0:1], mv[:, 1:2], ACT.Sqrt, bias=eps_c).then_inc(done, 1)

            def squares(b):
                nc.scalar.activation(sq[:, :, :], empty()[0:L, :, :], ACT.Square).then_inc(sq_ready, 1)

            def root(b):
                act.wait_ge(sqsum_ready, b + 1)
                nc.scalar.activation(sq[:, 0, :], sq[:, 1, :], ACT.Sqrt).then_inc(root_ready, 1)

            def x2T_of(b):
                copy(x2T[:, :, :], empty()[:, 0, 0:DC * L].rearrange("p (m l) -> p m l", m=DC))\
                    .then_inc(x2T_ready, 1)

            def sines(i, buf):
                act.wait_ge(angle_ready, i + 1)
                nc.scalar.activation(buf[:, :, :], buf[:, :, :], ACT.Sin).then_inc(ffn_w, 1)

            act.wait_ge(dve_const, 3)
            ln_sd(0, mv1, sd1, ln1_stat, ln1_sd)
            copy(xT[:, :, :], empty()[:, 1, 0:DC * L].rearrange("p (m l) -> p m l", m=DC))\
                .then_inc(xT_ready, 1)
            for i in range(NC // 2):
                ctxT_of(0, i)
            q_of(0)
            act.wait_ge(in_bias, 64)
            for m in range(DC):
                k_of(0, m)

            def one_pass(b, first, last):
                if first:
                    act.wait_ge(split_ready, 2)
                for g in range(DC):
                    for j in range(G):
                        if not first and g < DC - 1:
                            pT_of(b - 1, g + 1, j)
                        s_of(b, G * g + j)
                        if g == 0 and j == 0 and not last:
                            ln_sd(b + 1, mv1, sd1, ln1_stat, ln1_sd)
                        if g == DC - 1:
                            relu(b, j)
                    if not first and g < DC - 1:
                        mix_of(b - 1, g + 1)
                src = empty()
                if not first:
                    if last:
                        act.wait_ge(stored, 16 * (b - 1))
                    copy(att[:, :], src[0:L, 0, :]).then_inc(att_ready, 1)
                if not last:
                    copy(xT[:, :, :], src[:, 1, 0:DC * L].rearrange("p (m l) -> p m l", m=DC)).then_inc(xT_ready, 1)
                if first:
                    act.wait_ge(angle_step, 9)
                for i in range(NC // 2):
                    relu(b, G + i)
                    v_of(b, i)
                    if not last:
                        ctxT_of(b + 1, i)
                    if i == 1:
                        if first:
                            sines(0, wcos)
                            sines(1, wsin)
                        else:
                            ln_sd(b - 1, mv2, sd2, ln2_stat, ln2_sd)
                relu(b, G + 3)
                if not first:
                    x2T_of(b - 1)
                relu(b, 2 * G)
                relu(b, 2 * G + 1)
                if not last:
                    q_of(b + 1)
                relu(b, 2 * G + 2)
                relu(b, 2 * G + 3)
                if not first:
                    squares(b - 1)
                for m in range(DC):
                    pT_of(b, 0, m)
                    if not last:
                        k_of(b + 1, m)
                    relu(b, 3 * G + m)
                    if m == 1 and not first:
                        root(b - 1)
                mix_of(b, 0)

            passes(act, one_pass, ring)
            b = B - 1
            for g in range(1, DC):
                for j in range(G):
                    pT_of(b, g, j)
                mix_of(b, g)
            act.wait_ge(stored, 16 * (B - 1))
            copy(att[:, :], empty()[0:L, 0, :]).then_inc(att_ready, 1)
            ln_sd(b, mv2, sd2, ln2_stat, ln2_sd)
            x2T_of(b)
            squares(b)
            root(b)

        @block.vector
        def _(dve):
            FIND = G + G * (2 * TOP // 8 - 1)

            def layer_norm(b, src, in_wait, stats, mv, sd, dst, stat, sd_done, step, done):
                dve.sem_clear(step)
                in_wait()
                nc.vector.bn_stats(stats[:, :], src[:, :]).then_inc(step, 1)
                dve.wait_ge(step, 1)
                nc.vector.bn_aggr(mv[:, :], stats[:, :]).then_inc(stat, 1)
                dve.wait_ge(sd_done, b + 1)
                nc.vector.reciprocal(sd[:, 1:2], sd[:, 0:1]).then_inc(step, 1)
                dve.wait_ge(step, 2)
                nc.vector.tensor_scalar(dst[:, :], src[:, :], mv[:, 0:1], sd[:, 1:2],
                                        ALU.subtract, ALU.mult).then_inc(done, 1)

            def ln1(b):
                layer_norm(b, xq, lambda: dve.wait_ge(in_xq, 16 * (b + 1)), st1, mv1, sd1, xn,
                           ln1_stat, ln1_sd, ln1_step, xn_ready)

            def thresholds(b, g):
                base = step = 0
                dve.wait_ge(s_ready, H * b + G * (g + 1))
                dve.sem_inc(scores_seen, 1)
                dve.sem_clear(find)
                dve.sem_clear(tau_step)
                for j in range(G):
                    h = G * g + j
                    for i in range(PIECES):
                        last = nc.vector.max(cand[:, j, 8 * i:8 * i + 8], S[0:L, h, cuts[i]:cuts[i + 1]])
                    last.then_inc(find, 1)
                n = G
                for r in range(TOP // 8):
                    for j in range(G):
                        dve.wait_ge(find, base + n - G + j + 1)
                        nc.vector.max(top[:, j, 8 * r:8 * r + 8], cand[:, j, :]).then_inc(find, 1)
                    n += G
                    if r < TOP // 8 - 1:
                        for j in range(G):
                            dve.wait_ge(find, base + n - G + j + 1)
                            nc.vector.match_replace(cand[:, j, :], top[:, j, 8 * r:8 * r + 8], cand[:, j, :],
                                                    LOWEST).then_inc(find, 1)
                        n += G
                assert n == FIND
                dve.wait_ge(find, base + FIND)
                nc.vector.tensor_tensor(topz[:, :, :], top[:, :, :], top[:, :, 0:1].broadcast_to([L, G, TOP]),
                                        ALU.subtract).then_inc(tau_step, 1)
                dve.wait_ge(tau_step, step + 1)
                flat = lambda t: t[:, :, :].rearrange("p g k -> p (g k)")
                nc.vector.tensor_tensor_scan(flat(csum), flat(chain0), flat(topz), 0.0,
                                             ALU.mult, ALU.add).then_inc(tau_step, 1)
                dve.wait_ge(tau_step, step + 2)
                nc.vector.scalar_tensor_tensor(flat(gk), flat(csum), -1.0, flat(inv_k),
                                               ALU.add, ALU.mult).then_inc(tau_step, 1)
                dve.wait_ge(tau_step, step + 3)
                nc.vector.reduce_max(g_max[:, :], gk[:, :, :], AX).then_inc(tau_step, 1)
                dve.wait_ge(tau_step, step + 4)
                nc.vector.scalar_tensor_tensor(neg_tau[:, G * g:G * (g + 1)], g_max[:, :], -1.0, top[:, :, 0],
                                               ALU.mult, ALU.subtract).then_inc(tau_ready, 1)

            def newton(h, n):
                p = S[0:L, h, 0:N]
                nc.vector.tensor_scalar(scratch[:, :], p, 0.0, None, ALU.is_gt, ALU.add,
                                        accum_out=count[:, :]).then_inc(fix, 1)
                dve.wait_ge(fix, n + 1)
                nc.vector.tensor_scalar(scratch[:, :], p, 1.0, None, ALU.mult, ALU.add,
                                        accum_out=total[:, :]).then_inc(fix, 1)
                nc.vector.reciprocal(inv_count[:, :], count[:, :]).then_inc(fix, 1)
                dve.wait_ge(fix, n + 3)
                nc.vector.scalar_tensor_tensor(delta[:, :], total[:, :], -1.0, inv_count[:, :],
                                               ALU.add, ALU.mult).then_inc(fix, 1)
                dve.wait_ge(fix, n + 4)
                nc.vector.tensor_scalar(delta[:, :], delta[:, :], 0.0, None, ALU.max).then_inc(fix, 1)
                dve.wait_ge(fix, n + 5)
                nc.vector.tensor_scalar(p, p, delta[:, :], 0.0, ALU.subtract, ALU.max).then_inc(fix, 1)
                dve.wait_ge(fix, n + 6)
                return n + 6

            def refine(h):
                dve.sem_clear(fix)
                n = newton(h, 0)
                n = newton(h, n)
                nc.vector.tensor_scalar(scratch[:, :], S[0:L, h, 0:N], 1.0, None, ALU.mult, ALU.add,
                                        accum_out=total[:, :]).then_inc(fix, 1)
                dve.wait_ge(fix, n + 1)
                nc.vector.tensor_scalar(again[0:L, 0:1], total[:, :], 1.0 + SUM_TOL, None, ALU.is_gt).then_inc(fix, 1)
                dve.wait_ge(fix, n + 2)
                nc.vector.transpose(againT[:, :], again[:, :]).then_inc(fix, 1)
                dve.wait_ge(fix, n + 3)
                nc.vector.reduce_max(again_m[:, :], againT[:, :], AX).then_inc(fix, 1)
                dve.wait_ge(fix, n + 4)
                nc.vector.tensor_copy(again_i[:, :], again_m[:, :]).then_inc(fix, 1)
                dve.wait_ge(fix, n + 5)
                left = [dve.value_load(again_i[32 * q:32 * q + 1, 0:1], min_val=0, max_val=1) for q in range(P // 32)]
                with dve.If(left[0] + left[1] + left[2] + left[3] > 0):
                    with dve.Fori(0, NEWTON_MAX) as _:
                        dve.sem_clear(fix)
                        newton(h, 0)

            def mark(b, g):
                dve.wait_ge(relu_done, H * b + G * (g + 1))
                nc.vector.tensor_scalar(flag[:, 0:G], row_sum[:, G * g:G * (g + 1)], 1.0 + SUM_TOL, None,
                                        ALU.is_gt, ALU.add, accum_out=flag[:, G:G + 1]).then_inc(flag_ready, 1)

            def settle(b, g):
                dve.sem_clear(check_step)
                dve.wait_ge(flag_sum, DC * b + g + 1)
                nc.vector.tensor_copy(flag_i[:, :], flag_ps).then_inc(check_step, 1)
                dve.wait_ge(check_step, 1)
                with dve.If(dve.value_load(flag_i[0:1, G:G + 1], min_val=0, max_val=G * L) > 0):
                    for j in range(G):
                        with dve.If(dve.value_load(flag_i[0:1, j:j + 1], min_val=0, max_val=L) > 0):
                            refine(G * g + j)
                dve.sem_inc(verified, 1)

            def tail1(b):
                def x1_of():
                    dve.wait_ge(att_ready, b + 1)
                    dve.wait_ge(res_ready, b + 1)
                    nc.vector.tensor_tensor(x1[:, :], att[:, :], xr[:, :], ALU.add).then_inc(x1_ready, 1)
                    dve.wait_ge(x1_ready, b + 1)
                layer_norm(b, x1, x1_of, st2, mv2, sd2, x2n, ln2_stat, ln2_sd, ln2_step, x2n_ready)

            def tail2(b):
                dve.wait_ge(sq_ready, b + 1)
                nc.vector.tensor_tensor(sq[:, 1, :], sq[:, 0, :], sq[:, 1, :], ALU.add).then_inc(sqsum_ready, 1)
                dve.wait_ge(root_ready, b + 1)
                nc.vector.tensor_tensor(att[:, :], x1[:, :], sq[:, 0, :], ALU.add).then_inc(y_ready, 1)

            def angles(i, w, shift):
                n = [4 * i]
                turns = pT[:, :, :].rearrange("p g n -> p (g n)")[:, 0:DC * D].rearrange("p (c n) -> p c n", c=DC)

                def link(ins):
                    ins.then_inc(angle_step, 1)
                    n[0] += 1
                    dve.wait_ge(angle_step, n[0])

                n[0] = 8 * i
                link(nc.vector.tensor_tensor(w[:, :, :], w[:, :, :], v[:, 0:DC, :], ALU.add))
                link(nc.vector.tensor_scalar(turns, w[:, :, :], shift, 1.0 / TWO_PI, ALU.add, ALU.mult))
                link(nc.vector.tensor_scalar(turns, turns, ROUND, None, ALU.add))
                link(nc.vector.tensor_scalar(turns, turns, ROUND, None, ALU.subtract))
                link(nc.vector.scalar_tensor_tensor(w[:, :, :], turns, -TWO_PI_HI, w[:, :, :], ALU.mult, ALU.add))
                link(nc.vector.scalar_tensor_tensor(w[:, :, :], turns, -TWO_PI_LO, w[:, :, :], ALU.mult, ALU.add))
                link(nc.vector.tensor_scalar(w[:, :, :], w[:, :, :], shift, PI_BELOW, ALU.add, ALU.min))
                link(nc.vector.tensor_scalar(w[:, :, :], w[:, :, :], -PI_BELOW, None, ALU.max))
                dve.sem_inc(angle_ready, 1)

            nc.vector.memset(chain0[:, :, 1:TOP], 1.0)
            nc.vector.memset(chain0[:, :, 0:1], 0.0)
            nc.vector.memset(again[:, :], 0.0)
            for k in range(TOP):
                last = nc.vector.memset(inv_k[:, :, k:k + 1], 1.0 / (k + 1))
            last.then_inc(dve_const, 1)
            nc.vector.memset(eps_c, LN_EPS).then_inc(dve_const, 2)
            dve.wait_ge(dve_const, 3)
            ln1(0)
            for n, (w2, heads, loaded) in enumerate(((wk2, slice(0, DC), in_wk), (wv2, slice(DC, 2 * DC), in_wv))):
                dve.wait_ge(loaded, 16)
                nc.vector.tensor_scalar(w2[:, 0, :, :], S[:, heads, 0:D], W_SCALE, None,
                                        ALU.mult).then_inc(weight_step, 1)
                dve.wait_ge(weight_step, n + 1)
                nc.vector.scalar_tensor_tensor(w2[:, 1, :, :], S[:, heads, 0:D], W_SCALE, w2[:, 0, :, :],
                                               ALU.mult, ALU.subtract).then_inc(split_ready, 1)
            dve.wait_ge(in_angle, 48)
            angles(0, wcos, TWO_PI / 4)
            dve.wait_ge(in_angle, 64)
            angles(1, wsin, 0.0)

            def one_pass(b, first, last):
                if not first:
                    mark(b - 1, 3)
                if not last:
                    ln1(b + 1)
                if not first:
                    settle(b - 1, 3)
                thresholds(b, 0)
                thresholds(b, 1)
                mark(b, 0)
                thresholds(b, 2)
                if not first:
                    tail1(b - 1)
                settle(b, 0)
                mark(b, 1)
                thresholds(b, 3)
                settle(b, 1)
                mark(b, 2)
                if not first:
                    tail2(b - 1)
                settle(b, 2)

            passes(dve, one_pass)
            mark(B - 1, 3)
            settle(B - 1, 3)
            tail1(B - 1)
            tail2(B - 1)


_INS = ["x", "ctx_1024", "L0_xattn_Wq", "L0_xattn_bq", "L0_xattn_Wk", "L0_xattn_bk", "L0_xattn_Wv", "L0_xattn_bv",
        "L0_xattn_Wo", "L0_xattn_bo", "L0_ffn_theta", "L0_ffn_phi", "L0_ffn_theta_noise", "L0_ffn_phi_noise"]


def kernel(**inputs):
    import numpy as np
    import concourse.bacc as bacc
    from concourse.bass_utils import run_bass_kernel_spmd

    nc = bacc.Bacc("TRN2", target_bir_lowering=False, num_devices=1)
    arrays, args = {}, []
    for name in _INS:
        a = np.ascontiguousarray(inputs[name])
        arrays[f"in_{name}"] = a
        args.append(nc.dram_tensor(f"in_{name}", a.shape, mybir.dt.from_np(a.dtype), kind="ExternalInput").ap())
    args.append(nc.dram_tensor("out_y", inputs["x"].shape, F32, kind="ExternalOutput").ap())
    build_kernel(nc, *args)
    r = run_bass_kernel_spmd(nc, [arrays], core_ids=[0])
    return r.results[0]["out_y"]
```

```python
from contextlib import ExitStack

import concourse.bass as bass
from concourse import mybir

F32 = mybir.dt.float32
BF16 = mybir.dt.bfloat16
F16 = mybir.dt.float16
I32 = mybir.dt.int32
ALU = mybir.AluOpType
ACT = mybir.ActivationFunctionType
AX = mybir.AxisListType.X

P = 128
TWO_PI = 6.283185307179586
TWO_PI_HI = 6.28125
TWO_PI_LO = TWO_PI - TWO_PI_HI
ROUND = 1.5 * 2.0 ** 23
PI_BELOW = 3.1415925
W_SCALE = 64.0
LN_EPS = 1e-5
SUM_TOL = 1e-5
TOP = 48
PIECES = 12
NEWTON_MAX = 28
LOWEST = -3.0e38


class Ring:

    def __init__(self, per_pass):
        self.n, self.per_pass, self.passes = 0, per_pass, 0

    def take(self):
        n = self.n
        self.n += 1
        return n % 2, n, n + self.passes * self.per_pass if self.per_pass else n


def build_kernel(nc, x, ctx_in, Wq, bq, Wk, bk, Wv, bv, Wo, bo, theta, phi, theta_noise, phi_noise, out):
    B, L, D = x.shape
    N = ctx_in.shape[1]
    H = 16
    DH = D // H
    DC = D // P
    G = H // DC
    NC = -(-N // P)
    LAST = N - (NC - 1) * P
    HALF = N // 2
    TH = NC // 2 * L
    SCALE = float(DH) ** -0.5
    NCAND = 8 * PIECES
    cuts = [N * i // PIECES for i in range(PIECES + 1)]
    USES = H + 1 + NC // 2 + 1 + 1 + NC // 2 + 1 + DC

    assert D == DC * P and H == DC * G and N == 2 * HALF and NC % 2 == 0 and USES % 2 == 0

    es = ExitStack()
    with es:
        def sb(name, shape, dt=F32):
            return es.enter_context(nc.sbuf_tensor(name, shape, dt))

        def sem(name):
            return es.enter_context(nc.semaphore(name))

        wq, wo = sb("wq", [P, DC, D]), sb("wo", [P, DC, D])
        wk2, wv2 = sb("wk2", [P, 2, DC, D], F16), sb("wv2", [P, 2, DC, D], F16)
        wcos, wsin = sb("wcos", [P, DC, D]), sb("wsin", [P, DC, D])
        ctx_nat = sb("ctx_nat", [P, NC, D])
        ctxT2 = sb("ctxT2", [P, 2, DC, NC * P], F16)
        ctxT_f = sb("ctxT_f", [P, DC, 2 * P])
        kT2 = sb("kT2", [P, 2, DC, N], F16)
        k_f = sb("k_f", [P, 2, N])
        v = sb("v", [P, NC, D])
        S = sb("S", [P, H, NC * P])
        pT = sb("pT", [P, G, NC * L])
        qz2 = sb("qz2", [P, 2, DC, G, L], F16)
        q_raw = sb("q_raw", [P, DC, L])
        aT = sb("aT", [P, DC, L])
        xT, x2T = sb("xT", [P, DC, L]), sb("x2T", [P, DC, L])
        ident = sb("ident", [P, P])
        ones = sb("ones", [P, 1])
        bk_c, bq_c, bv_c = sb("bk_c", [P, DC]), sb("bq_c", [P, DC]), sb("bv_c", [P, DC])
        bo_b = sb("bo_b", [L, D])
        xq, xr, xn, x1, x2n, att = (sb(n, [L, D]) for n in ("xq", "xr", "xn", "x1", "x2n", "att"))
        sq = sb("sq", [L, 2, D])
        cand = sb("cand", [L, G, NCAND])
        top = sb("top", [L, G, TOP])
        topz, csum, gk = (sb(n, [L, G, TOP]) for n in ("topz", "csum", "gk"))
        chain0, inv_k = sb("chain0", [L, G, TOP]), sb("inv_k", [L, G, TOP])
        g_max = sb("g_max", [L, G])
        neg_tau = sb("neg_tau", [L, H])
        row_sum = sb("row_sum", [L, H])
        flag = sb("flag", [L, 2 * G])
        bit, flag_bits = sb("bit", [1, 2 * G]), sb("flag_bits", [1, 2 * G])
        flag_code, flag_i = sb("flag_code", [1, 1]), sb("flag_i", [1, 1], I32)
        again = sb("again", [P, 32])
        againT = sb("againT", [P, 32])
        again_m = sb("again_m", [P, 1])
        again_i = sb("again_i", [P, 1], I32)
        count, inv_count, new_sum, delta = (sb(n, [L, 1]) for n in ("count", "inv_count", "new_sum", "delta"))
        eps_t = sb("eps_t", [L, 1])
        eps_c = eps_t[:, :]
        scratch = cand[:, :, :].rearrange("p g n -> p (g n)").bitcast(BF16)[:, 0:N]
        st1, mv1, sd1 = sb("st1", [L, 6]), sb("mv1", [L, 2]), sb("sd1", [L, 2])
        st2, mv2, sd2 = sb("st2", [L, 6]), sb("mv2", [L, 2]), sb("sd2", [L, 2])

        work = es.enter_context(nc.psum_tensor("work", [P, 2, 2, 512], F32))
        tps = es.enter_context(nc.psum_tensor("tps", [P, 2, 512], F32))
        mix_bank = es.enter_context(nc.psum_tensor("mix_bank", [P, 512], F32))
        flag_bank = es.enter_context(nc.psum_tensor("flag_bank", [P, 512], F32))
        mix_ps, flag_ps = mix_bank[:, 0:L], flag_bank[0:1, 0:2 * G]

        in_ctx, in_xq, in_xr = sem("in_ctx"), sem("in_xq"), sem("in_xr")
        in_wk, in_wq, in_wv, in_wo = sem("in_wk"), sem("in_wq"), sem("in_wv"), sem("in_wo")
        in_bias, in_angle = sem("in_bias"), sem("in_angle")
        stored, store_seen = sem("stored"), sem("store_seen")
        pad_zero, ident0, const_ready, bq_scaled = (sem("pad_zero"), sem("ident0"), sem("const_ready"), sem("bq_scaled"))
        dve_const, angle_step = sem("dve_const"), sem("angle_step")
        angle_ready, ffn_w = sem("angle_ready"), sem("ffn_w")
        work_full = sem("work_full")
        weight_step, split_ready = sem("weight_step"), sem("split_ready")
        ctx_f_ready, k_f_ready, q_sum = sem("ctx_f_ready"), sem("k_f_ready"), sem("q_sum")
        ctx_lo_ready, k_lo_ready = sem("ctx_lo_ready"), sem("k_lo_ready")
        xT_ready, q_raw_ready, qz_ready = (sem(n) for n in ("xT_ready", "q_raw_ready", "qz_ready"))
        v_ready = sem("v_ready")
        s_ready, tau_ready, relu_done = sem("s_ready"), sem("tau_ready"), sem("relu_done")
        flag_ready, flag_sum, verified = sem("flag_ready"), sem("flag_sum"), sem("verified")
        pT_full, pT_ready, mix_full, mix_read = (sem(n) for n in ("pT_full", "pT_ready", "mix_full", "mix_read"))
        att_ready, x1_ready, res_ready = (sem(n) for n in ("att_ready", "x1_ready", "res_ready"))
        find, tau_step, check_step, fix = sem("find"), sem("tau_step"), sem("check_step"), sem("fix")
        scores_seen = sem("scores_seen")
        ln1_stat, ln1_sd, ln1_step, xn_ready = (sem(n) for n in ("ln1_stat", "ln1_sd", "ln1_step", "xn_ready"))
        ln2_stat, ln2_sd, ln2_step, x2n_ready = (sem(n) for n in ("ln2_stat", "ln2_sd", "ln2_step", "x2n_ready"))
        x2T_ready, sq_ready, sqsum_ready, root_ready, y_ready = (
            sem(n) for n in ("x2T_ready", "sq_ready", "sqsum_ready", "root_ready", "y_ready"))

        block = es.enter_context(nc.Block())

        def passes(eng, one_pass, ring=None):
            one_pass(0, True, False)
            if ring:
                ring.passes = 0
                start = ring.n
            with eng.Fori(1, B - 1) as b:
                if ring:
                    ring.passes = b - 1
                one_pass(b, False, False)
            if ring:
                ring.passes = 0
                assert ring.n - start == ring.per_pass
                ring.n = start + (B - 2) * ring.per_pass
            one_pass(B - 1, False, True)

        @block.sync
        def _(sp):
            def load_ctx(b):
                sp.wait_ge(ctx_f_ready, NC // 2 * b)
                src = ctx_in[bass.ds(b, 1), :, :]
                sp.dma_start(ctx_nat[:, 0:NC - 1, :],
                             src[:, 0:(NC - 1) * P, :].rearrange("a (c p) d -> p (a c) d", p=P)).then_inc(in_ctx, 16)
                sp.dma_start(ctx_nat[0:LAST, NC - 1, :],
                             src[:, (NC - 1) * P:N, :].rearrange("a p d -> p (a d)")).then_inc(in_ctx, 16)

            def load_x(buf, b, done):
                sp.dma_start(buf[:, :], x[bass.ds(b, 1), :, :].rearrange("a l d -> l (a d)")).then_inc(done, 16)

            def weight(dst, src, done):
                sp.dma_start(dst, src.rearrange("(c p) n -> p c n", p=P)).then_inc(done, 16)

            load_x(xq, 0, in_xq)
            sp.wait_ge(pad_zero, 1)
            load_ctx(0)
            for dst, src in ((bq_c, bq), (bk_c, bk), (bv_c, bv)):
                sp.dma_start(dst[:, :], src.rearrange("(m p) -> p m", p=P),
                             allow_slow_non_contiguous=True).then_inc(in_bias, 16)
            sp.dma_start(bo_b[:, :], bo.rearrange("(a n) -> a n", a=1).broadcast_to([L, D])).then_inc(in_bias, 16)
            weight(wq[:, :, :], Wq, in_wq)
            weight(S[:, 0:DC, 0:D], Wk, in_wk)
            weight(S[:, DC:2 * DC, 0:D], Wv, in_wv)
            weight(wcos[:, :, :], theta, in_angle)
            weight(v[:, 0:DC, :], theta_noise, in_angle)
            weight(wsin[:, :, :], phi, in_angle)
            weight(wo[:, :, :], Wo, in_wo)
            sp.wait_ge(xn_ready, 1)
            load_x(xq, 1, in_xq)
            sp.wait_ge(angle_step, 1)
            weight(v[:, 0:DC, :], phi_noise, in_angle)

            def one_pass(b, first, last):
                if not last:
                    if not first:
                        sp.wait_ge(xn_ready, b + 1)
                        load_x(xq, b + 1, in_xq)
                    load_ctx(b + 1)
                if first:
                    load_x(xr, 0, in_xr)
                else:
                    sp.wait_ge(x1_ready, b)
                    load_x(xr, b, in_xr)
                if not first:
                    store(b - 1)
                    sp.wait_ge(stored, 16 * b)
                    sp.sem_inc(store_seen, 1)

            def store(b):
                sp.wait_ge(y_ready, b + 1)
                sp.dma_start(out[bass.ds(b, 1), :, :].rearrange("a l d -> l (a d)"), att[:, :]).then_inc(stored, 16)

            passes(sp, one_pass)
            store(B - 1)
            sp.wait_ge(stored, 16 * B)

        @block.gpsimd
        def _(pool):
            pool.memset(ctx_nat[64:P, NC - 1, :], 0.0).then_inc(pad_zero, 1)
            pool.wait_ge(pad_zero, 1)
            pool.memset(S[:, :, N:NC * P], 0.0).then_inc(pad_zero, 1)
            pool.wait_ge(pad_zero, 2)
            pool.memset(ident[:, :], 0.0).then_inc(ident0, 1)
            pool.wait_ge(ident0, 1)
            pool.affine_select(out=ident[:, :], in_=ident[:, :], compare_op=ALU.not_equal, fill=1.0,
                               base=0, pattern=[[-1, P]], channel_multiplier=1).then_inc(const_ready, 1)
            pool.wait_ge(const_ready, 1)
            pool.memset(ones[:, :], 1.0).then_inc(const_ready, 1)
            pool.wait_ge(const_ready, 2)
            pool.memset(qz2[:, :, :, :, :], 0.0).then_inc(const_ready, 1)
            pool.wait_ge(const_ready, 3)
            pool.wait_ge(in_bias, 64)
            pool.tensor_scalar(bq_c[:, :], bq_c[:, :], SCALE, None, ALU.mult).then_inc(bq_scaled, 1)
            pool.wait_ge(bq_scaled, 1)

            def pad_q(b):
                pool.wait_ge(q_raw_ready, b + 1)
                for j in range(G):
                    r = slice(DH * j, DH * (j + 1))
                    pool.tensor_tensor(qz2[r, 0, :, j, :], q_raw[r, :, :],
                                       bq_c[r, :].rearrange("p (m a) -> p m a", a=1).broadcast_to([DH, DC, L]),
                                       ALU.add).then_inc(qz_ready, 1)
                    pool.wait_ge(qz_ready, 2 * G * b + j + 1)
                pool.tensor_tensor(q_raw[:, :, :], q_raw[:, :, :],
                                   bq_c[:, :].rearrange("p (m a) -> p m a", a=1).broadcast_to([P, DC, L]),
                                   ALU.add).then_inc(q_sum, 1)
                pool.wait_ge(q_sum, b + 1)
                for j in range(G):
                    r = slice(DH * j, DH * (j + 1))
                    pool.tensor_tensor(qz2[r, 1, :, j, :], q_raw[r, :, :], qz2[r, 0, :, j, :],
                                       ALU.subtract).then_inc(qz_ready, 1)
                    pool.wait_ge(qz_ready, 2 * G * b + G + j + 1)

            def low_ctx(b, i):
                pool.wait_ge(ctx_f_ready, NC // 2 * b + i + 1)
                at = slice(2 * i * P, 2 * (i + 1) * P)
                pool.tensor_tensor(ctxT2[:, 1, :, at], ctxT_f[:, :, :], ctxT2[:, 0, :, at],
                                   ALU.subtract).then_inc(ctx_lo_ready, 1)
                pool.wait_ge(ctx_lo_ready, NC // 2 * b + i + 1)

            def low_k(b, m):
                pool.wait_ge(k_f_ready, DC * b + m + 1)
                pool.tensor_tensor(kT2[:, 1, m, :], k_f[:, m % 2, :], kT2[:, 0, m, :],
                                   ALU.subtract).then_inc(k_lo_ready, 1)
                pool.wait_ge(k_lo_ready, DC * b + m + 1)

            def prepare(b):
                for i in range(NC // 2):
                    low_ctx(b, i)
                pad_q(b)
                for m in range(DC):
                    low_k(b, m)

            def residual(b):
                pool.wait_ge(in_xr, 16 * (b + 1))
                pool.tensor_tensor(xr[:, :], xr[:, :], bo_b[:, :], ALU.add).then_inc(res_ready, 1)
                pool.wait_ge(res_ready, b + 1)

            prepare(0)

            def one_pass(b, first, last):
                if not last:
                    prepare(b + 1)
                residual(b)

            passes(pool, one_pass)

        @block.tensor
        def _(pe):
            ring = Ring(USES)

            def take():
                return work[:, ring.take()[0], :, :]

            def transpose_x(src, psum):
                for c in range(DC):
                    last = nc.tensor.transpose(psum[:, c * L:(c + 1) * L], src[:, c * P:(c + 1) * P], ident[0:L, 0:L])
                return last

            def project2(psum, lhs, w):
                terms = [(c, i, j) for c in range(DC) for i, j in ((0, 0), (0, 1), (1, 0))]
                for n, (c, i, j) in enumerate(terms):
                    last = nc.tensor.matmul(psum, lhs(c, i), w(c, j), start=(n == 0), stop=(n == len(terms) - 1))
                return last

            def project(psum, lhs, w):
                for c in range(DC):
                    last = nc.tensor.matmul(psum, lhs(c), w(c), start=(c == 0), stop=(c == DC - 1))
                return last

            def q_of(b, before_v=False):
                pe.wait_ge(xT_ready, b + 1)
                if before_v:
                    pe.wait_ge(ctx_f_ready, NC // 2 - 1)
                else:
                    pe.wait_ge(v_ready, NC // 2 * b)
                buf = take()
                for m in range(DC):
                    last = project(buf[:, 0, m * L:(m + 1) * L],
                                   lambda c: wq[:, c, m * P:(m + 1) * P], lambda c: xT[:, c, :])
                last.then_inc(work_full, 1)

            def transpose_ctx(b, i, att_before=0, v_between=True):
                if i > 0 and not v_between:
                    if i > 1:
                        pe.wait_ge(ctx_f_ready, i - 1)
                    else:
                        pe.wait_ge(xT_ready, 1)
                elif i > 0:
                    pe.wait_ge(ctx_f_ready, NC // 2 * b + i)
                else:
                    pe.wait_ge(in_ctx, 32 * (b + 1))
                    pe.wait_ge(xT_ready, b + 1)
                    if att_before is not None:
                        pe.wait_ge(att_ready, att_before)
                buf = take()
                for j in range(2):
                    for c in range(DC):
                        last = nc.tensor.transpose(buf[:, j, c * P:(c + 1) * P],
                                                   ctx_nat[:, 2 * i + j, c * P:(c + 1) * P], ident[:, :])
                last.then_inc(work_full, 1)

            def k_of(b, m, squares_before=None):
                if m == 0:
                    pe.wait_ge(ctx_lo_ready, NC // 2 * (b + 1))
                if m == (1 if squares_before is None else 0):
                    pe.wait_ge(q_raw_ready, b + 1)
                elif m == 2 and squares_before is not None:
                    pe.wait_ge(sq_ready, squares_before)
                elif m > 0:
                    pe.wait_ge(k_f_ready, DC * b + (m - 1 if squares_before is None or m > 1 else 1))
                buf = take()
                for half in range(2):
                    last = project2(buf[:, half, 0:HALF], lambda c, i: wk2[:, i, c, m * P:(m + 1) * P],
                                    lambda c, j: ctxT2[:, j, c, half * HALF:(half + 1) * HALF])
                last.then_inc(work_full, 1)

            def v_of(b, i, last_pass):
                if i == 0:
                    pe.wait_ge(s_ready, H * (b + 1))
                else:
                    pe.wait_ge(v_ready, NC // 2 * b + i)
                    if last_pass:
                        pe.wait_ge(att_ready, b)
                buf = take()
                for j in range(2):
                    kc = 2 * i + j
                    last = project2(buf[:, j, :], lambda c, i: ctxT2[:, i, c, kc * P:(kc + 1) * P],
                                    lambda c, j: wv2[:, j, c, :])
                last.then_inc(work_full, 1)

            def scores(b, h):
                if h % G == 0:
                    pe.wait_ge(k_lo_ready, DC * b + h // G + 1)
                if h < 2:
                    pe.wait_ge(k_f_ready, DC * (b + 1) - 1 + h)
                else:
                    pe.wait_ge(s_ready, H * b + h - 1)
                buf = take()
                for half in range(2):
                    for n, (i, j) in enumerate(((0, 0), (0, 1), (1, 0))):
                        last = nc.tensor.matmul(buf[0:L, half, 0:HALF], qz2[:, i, h // G, h % G, :],
                                                kT2[:, j, h // G, half * HALF:(half + 1) * HALF],
                                                start=(n == 0), stop=(n == 2))
                last.then_inc(work_full, 1)

            def transpose_p(b, g, j):
                if j == 0:
                    pe.wait_ge(verified, 2 * b + g // 2 + 1)
                h = G * g + j
                for half in range(2):
                    if j > 0:
                        pe.wait_ge(pT_ready, 2 * (H * b + h) + half - 1)
                    for c in range(NC // 2):
                        kc = half * NC // 2 + c
                        last = nc.tensor.transpose(tps[:, half, c * L:(c + 1) * L],
                                                   S[0:L, h, kc * P:(kc + 1) * P], ident[0:L, 0:L])
                    last.then_inc(pT_full, 1)

            def mix(b, g):
                pe.wait_ge(pT_ready, 2 * (H * b + G * (g + 1)))
                if g == 0:
                    pe.wait_ge(v_ready, NC // 2 * (b + 1))
                else:
                    pe.wait_ge(mix_read, DC * b + g)
                for kc in range(NC):
                    for j in range(G):
                        h = G * g + j
                        last = nc.tensor.matmul(mix_ps[DH * j:DH * (j + 1), :], v[:, kc, DH * h:DH * (h + 1)],
                                                pT[:, j, kc * L:(kc + 1) * L],
                                                start=(kc == 0), stop=(kc == NC - 1))
                last.then_inc(mix_full, 1)

            def sum_flags(b, part):
                pe.wait_ge(flag_ready, 2 * b + part + 1)
                nc.tensor.matmul(flag_ps, ones[0:L, :], flag[:, :], start=True, stop=True).then_inc(flag_sum, 1)

            def o_part(b, c, buf):
                pe.wait_ge(mix_read, DC * b + c + 1)
                return nc.tensor.matmul(buf[0:L, 0, :], aT[:, c, :], wo[:, c, :], start=(c == 0), stop=(c == DC - 1))

            def o_of(b, buf):
                return [o_part(b, c, buf) for c in range(DC)][-1]

            def xT_of(b, buf):
                pe.wait_ge(xn_ready, b + 1)
                return transpose_x(xn, buf[:, 1, :])

            def x2T_of(b, sem_before, value):
                pe.wait_ge(sem_before, value)
                pe.wait_ge(x2n_ready, b + 1)
                transpose_x(x2n, take()[:, 0, :]).then_inc(work_full, 1)

            def ffn_of(b, sem_before, value):
                pe.wait_ge(sem_before, value)
                pe.wait_ge(x2T_ready, b + 1)
                buf = take()
                project(buf[0:L, 0, :], lambda c: x2T[:, c, :], lambda c: wcos[:, c, :])
                project(buf[0:L, 1, :], lambda c: x2T[:, c, :], lambda c: wsin[:, c, :]).then_inc(work_full, 1)

            pe.wait_ge(const_ready, 3)
            xT_of(0, take()).then_inc(work_full, 1)
            for i in range(NC // 2):
                transpose_ctx(0, i, None, False)
            pe.wait_ge(in_wq, 16)
            q_of(0, True)
            pe.wait_ge(split_ready, 1)
            for m in range(DC):
                k_of(0, m)
            pe.wait_ge(split_ready, 2)

            def one_pass(b, first, last):
                pe.wait_ge(qz_ready, 2 * G * (b + 1))
                for g in range(DC):
                    for j in range(G):
                        if not first:
                            transpose_p(b - 1, g, j)
                        scores(b, G * g + j)
                        if g == 0 and j == 0 and not first:
                            sum_flags(b - 1, 1)
                    if not first:
                        mix(b - 1, g)
                pe.wait_ge(s_ready, H * (b + 1) - 1)
                buf = take()
                if first:
                    pe.wait_ge(in_wo, 16)
                else:
                    end = o_of(b - 1, buf)
                if not last:
                    end = xT_of(b + 1, buf)
                end.then_inc(work_full, 1)
                for i in range(NC // 2):
                    v_of(b, i, last)
                    if not last:
                        transpose_ctx(b + 1, i, None if first else b)
                if not last:
                    q_of(b + 1)
                if first:
                    for m in range(DC):
                        k_of(b + 1, m)
                    sum_flags(b, 0)
                else:
                    if last:
                        x2T_of(b - 1, v_ready, NC // 2 * (b + 1) - 1)
                    else:
                        x2T_of(b - 1, ctx_f_ready, NC // 2 * (b + 2))
                        k_of(b + 1, 0, b)
                    pe.wait_ge(ffn_w, 2)
                    ffn_of(b - 1, v_ready, NC // 2 * (b + 1))
                    sum_flags(b, 0)
                    if not last:
                        for m in range(1, DC):
                            k_of(b + 1, m, b)

            passes(pe, one_pass, ring)
            b = B - 1
            pe.wait_ge(x2T_ready, b)
            o_buf = take()
            for g in range(DC):
                if g == 1:
                    sum_flags(b, 1)
                for j in range(G):
                    transpose_p(b, g, j)
                mix(b, g)
                if g > 0:
                    o_part(b, g - 1, o_buf)
            o_part(b, DC - 1, o_buf).then_inc(work_full, 1)
            x2T_of(b, sq_ready, b)
            ffn_of(b, att_ready, b + 1)

        @block.scalar
        def _(act):
            ring = Ring(USES)

            def empty():
                slot, n, count_now = ring.take()
                act.wait_ge(work_full, count_now + 1)
                return work[:, slot, :, :]

            def at_start(b):
                return isinstance(b, int) and b == 0

            def copy(dst, src, **kw):
                return nc.scalar.activation(dst, src, ACT.Copy, **kw)

            def q_of(b):
                copy(q_raw[:, :, :], empty()[:, 0, 0:DC * L].rearrange("p (m l) -> p m l", m=DC),
                     scale=SCALE).then_inc(q_raw_ready, 1)

            def ctxT_of(b, i):
                src = empty()
                for part, dst in ((0, ctxT2[:, 0, :, 2 * i * P:2 * (i + 1) * P]), (1, ctxT_f[:, :, :])):
                    if part == 1 and (i > 0 or not at_start(b)):
                        act.wait_ge(ctx_lo_ready, NC // 2 * b + i)
                    for j in range(2):
                        last = copy(dst[:, :, j * P:(j + 1) * P], src[:, j, :].rearrange("p (c k) -> p c k", c=DC))
                last.then_inc(ctx_f_ready, 1)

            def k_of(b, m):
                src = empty()
                for part, dst in enumerate((kT2[:, 0, m, :], k_f[:, m % 2, :])):
                    if part == 1 and (m > 1 or not at_start(b)):
                        act.wait_ge(k_lo_ready, DC * b + m - 1)
                    last = nc.scalar.activation(dst.rearrange("p (a n) -> p a n", a=2), src[:, :, 0:HALF],
                                                ACT.Identity, bias=bk_c[:, m:m + 1], scale=1.0 / W_SCALE)
                last.then_inc(k_f_ready, 1)

            def v_of(b, i):
                copy(v[:, 2 * i:2 * i + 2, :], empty()[:, :, :], scale=1.0 / W_SCALE).then_inc(v_ready, 1)

            def s_of(b, h):
                copy(S[0:L, h, 0:N].rearrange("p (a n) -> p a n", a=2),
                     empty()[0:L, :, 0:HALF]).then_inc(s_ready, 1)

            def relu(b, h):
                if h % G == 0:
                    act.wait_ge(tau_ready, DC * b + h // G + 1)
                nc.scalar.activation(S[0:L, h, 0:N], S[0:L, h, 0:N], ACT.Relu, bias=neg_tau[:, h:h + 1],
                                     accum_out=row_sum[:, h:h + 1]).then_inc(relu_done, 1)

            def pT_of(b, g, j):
                if g > 0:
                    act.wait_ge(mix_full, DC * b + g)
                for half in range(2):
                    act.wait_ge(pT_full, 2 * (H * b + G * g + j) + half + 1)
                    copy(pT[:, j, half * TH:(half + 1) * TH], tps[:, half, 0:TH]).then_inc(pT_ready, 1)

            def mix_of(b, g):
                act.wait_ge(mix_full, DC * b + g + 1)
                nc.scalar.activation(aT[:, g, :], mix_ps, ACT.Identity, bias=bv_c[:, g:g + 1]).then_inc(mix_read, 1)

            def ln_sd(b, mv, sd, stat, done):
                act.wait_ge(stat, b + 1)
                nc.scalar.activation(sd[:, 0:1], mv[:, 1:2], ACT.Sqrt, bias=eps_c).then_inc(done, 1)

            def squares(b):
                nc.scalar.activation(sq[:, :, :], empty()[0:L, :, :], ACT.Square).then_inc(sq_ready, 1)

            def root(b):
                act.wait_ge(sqsum_ready, b + 1)
                nc.scalar.activation(sq[:, 0, :], sq[:, 1, :], ACT.Sqrt).then_inc(root_ready, 1)

            def x2T_of(b):
                copy(x2T[:, :, :], empty()[:, 0, 0:DC * L].rearrange("p (m l) -> p m l", m=DC))\
                    .then_inc(x2T_ready, 1)

            def sines(i, buf):
                act.wait_ge(angle_ready, i + 1)
                nc.scalar.activation(buf[:, :, :], buf[:, :, :], ACT.Sin).then_inc(ffn_w, 1)

            act.wait_ge(dve_const, 3)
            ln_sd(0, mv1, sd1, ln1_stat, ln1_sd)
            copy(xT[:, :, :], empty()[:, 1, 0:DC * L].rearrange("p (m l) -> p m l", m=DC))\
                .then_inc(xT_ready, 1)
            for i in range(NC // 2):
                ctxT_of(0, i)
            q_of(0)
            ln_sd(1, mv1, sd1, ln1_stat, ln1_sd)
            act.wait_ge(in_bias, 64)
            for m in range(DC):
                k_of(0, m)

            def one_pass(b, first, last):
                if first:
                    act.wait_ge(split_ready, 2)
                for g in range(DC):
                    for j in range(G):
                        if not first:
                            pT_of(b - 1, g, j)
                        s_of(b, G * g + j)
                        if g == 0 and j == 0 and not first and not last:
                            ln_sd(b + 1, mv1, sd1, ln1_stat, ln1_sd)
                        if g == DC - 1 and not first:
                            relu(b, j)
                    if not first:
                        mix_of(b - 1, g)
                src = empty()
                if not first:
                    if last:
                        act.wait_ge(stored, 16 * (b - 1))
                    copy(att[:, :], src[0:L, 0, :]).then_inc(att_ready, 1)
                if not last:
                    copy(xT[:, :, :], src[:, 1, 0:DC * L].rearrange("p (m l) -> p m l", m=DC)).then_inc(xT_ready, 1)
                if first:
                    act.wait_ge(angle_step, 9)
                for i in range(NC // 2):
                    if not first:
                        relu(b, G + i)
                    v_of(b, i)
                    if not last:
                        ctxT_of(b + 1, i)
                    if first:
                        relu(b, i)
                    if i == 1 and first:
                        sines(0, wcos)
                        sines(1, wsin)
                if first:
                    relu(b, G - 1)
                    q_of(b + 1)
                    for m in range(DC):
                        k_of(b + 1, m)
                        relu(b, G + m)
                    for h in range(2 * G, H):
                        relu(b, h)
                else:
                    ln_sd(b - 1, mv2, sd2, ln2_stat, ln2_sd)
                    relu(b, 2 * G - 1)
                    if not last:
                        q_of(b + 1)
                    relu(b, 2 * G)
                    x2T_of(b - 1)
                    relu(b, 2 * G + 1)
                    if not last:
                        k_of(b + 1, 0)
                    relu(b, 2 * G + 2)
                    relu(b, 2 * G + 3)
                    squares(b - 1)
                    root(b - 1)
                    for m in range(1, DC):
                        relu(b, 3 * G + m - 1)
                        if m == DC - 1:
                            relu(b, 3 * G + m)
                        if not last:
                            k_of(b + 1, m)

            passes(act, one_pass, ring)
            b = B - 1
            for g in range(DC):
                for j in range(G):
                    pT_of(b, g, j)
                mix_of(b, g)
            act.wait_ge(stored, 16 * (B - 1))
            copy(att[:, :], empty()[0:L, 0, :]).then_inc(att_ready, 1)
            ln_sd(b, mv2, sd2, ln2_stat, ln2_sd)
            x2T_of(b)
            squares(b)
            root(b)

        @block.vector
        def _(dve):
            FIND = G + G * (2 * TOP // 8 - 1)

            def layer_norm(b, src, in_wait, stats, mv, sd, dst, stat, sd_done, step, done):
                dve.sem_clear(step)
                in_wait()
                nc.vector.bn_stats(stats[:, :], src[:, :]).then_inc(step, 1)
                dve.wait_ge(step, 1)
                nc.vector.bn_aggr(mv[:, :], stats[:, :]).then_inc(stat, 1)
                dve.wait_ge(sd_done, b + 1)
                nc.vector.reciprocal(sd[:, 1:2], sd[:, 0:1]).then_inc(step, 1)
                dve.wait_ge(step, 2)
                nc.vector.tensor_scalar(dst[:, :], src[:, :], mv[:, 0:1], sd[:, 1:2],
                                        ALU.subtract, ALU.mult).then_inc(done, 1)

            def ln1(b):
                layer_norm(b, xq, lambda: dve.wait_ge(in_xq, 16 * (b + 1)), st1, mv1, sd1, xn,
                           ln1_stat, ln1_sd, ln1_step, xn_ready)

            def thresholds(b, g):
                base = step = 0
                dve.wait_ge(s_ready, H * b + G * (g + 1))
                dve.sem_inc(scores_seen, 1)
                dve.sem_clear(find)
                dve.sem_clear(tau_step)
                for j in range(G):
                    h = G * g + j
                    for i in range(PIECES):
                        last = nc.vector.max(cand[:, j, 8 * i:8 * i + 8], S[0:L, h, cuts[i]:cuts[i + 1]])
                    last.then_inc(find, 1)
                n = G
                for r in range(TOP // 8):
                    for j in range(G):
                        dve.wait_ge(find, base + n - G + j + 1)
                        nc.vector.max(top[:, j, 8 * r:8 * r + 8], cand[:, j, :]).then_inc(find, 1)
                    n += G
                    if r < TOP // 8 - 1:
                        for j in range(G):
                            dve.wait_ge(find, base + n - G + j + 1)
                            nc.vector.match_replace(cand[:, j, :], top[:, j, 8 * r:8 * r + 8], cand[:, j, :],
                                                    LOWEST).then_inc(find, 1)
                        n += G
                assert n == FIND
                dve.wait_ge(find, base + FIND)
                nc.vector.tensor_tensor(topz[:, :, :], top[:, :, :], top[:, :, 0:1].broadcast_to([L, G, TOP]),
                                        ALU.subtract).then_inc(tau_step, 1)
                dve.wait_ge(tau_step, step + 1)
                flat = lambda t: t[:, :, :].rearrange("p g k -> p (g k)")
                nc.vector.tensor_tensor_scan(flat(csum), flat(chain0), flat(topz), 0.0,
                                             ALU.mult, ALU.add).then_inc(tau_step, 1)
                dve.wait_ge(tau_step, step + 2)
                nc.vector.scalar_tensor_tensor(flat(gk), flat(csum), -1.0, flat(inv_k),
                                               ALU.add, ALU.mult).then_inc(tau_step, 1)
                dve.wait_ge(tau_step, step + 3)
                nc.vector.reduce_max(g_max[:, :], gk[:, :, :], AX).then_inc(tau_step, 1)
                dve.wait_ge(tau_step, step + 4)
                nc.vector.scalar_tensor_tensor(neg_tau[:, G * g:G * (g + 1)], g_max[:, :], -1.0, top[:, :, 0],
                                               ALU.mult, ALU.subtract).then_inc(tau_ready, 1)

            def newton(h, n, total):
                p = S[0:L, h, 0:N]
                nc.vector.tensor_scalar(scratch[:, :], p, 0.0, None, ALU.is_gt, ALU.add,
                                        accum_out=count[:, :]).then_inc(fix, 1)
                dve.wait_ge(fix, n + 1)
                nc.vector.reciprocal(inv_count[:, :], count[:, :]).then_inc(fix, 1)
                dve.wait_ge(fix, n + 2)
                nc.vector.scalar_tensor_tensor(delta[:, :], total, -1.0, inv_count[:, :],
                                               ALU.add, ALU.mult).then_inc(fix, 1)
                dve.wait_ge(fix, n + 3)
                nc.vector.tensor_scalar(delta[:, :], delta[:, :], 0.0, None, ALU.max).then_inc(fix, 1)
                dve.wait_ge(fix, n + 4)
                nc.vector.scalar_tensor_tensor(p, p, delta[:, :], chain0[:, 0, 0:1].broadcast_to([L, N]),
                                               ALU.subtract, ALU.max, accum_out=new_sum[:, :]).then_inc(fix, 1)
                dve.wait_ge(fix, n + 5)
                return n + 5

            def refine(h):
                dve.sem_clear(fix)
                n = newton(h, 0, row_sum[:, h:h + 1])
                n = newton(h, n, new_sum[:, :])
                nc.vector.tensor_scalar(again[0:L, 0:1], new_sum[:, :], 1.0 + SUM_TOL, None, ALU.is_gt).then_inc(fix, 1)
                dve.wait_ge(fix, n + 1)
                nc.vector.transpose(againT[:, :], again[:, :]).then_inc(fix, 1)
                dve.wait_ge(fix, n + 2)
                nc.vector.reduce_max(again_m[:, :], againT[:, :], AX).then_inc(fix, 1)
                dve.wait_ge(fix, n + 3)
                nc.vector.tensor_copy(again_i[:, :], again_m[:, :]).then_inc(fix, 1)
                dve.wait_ge(fix, n + 4)
                left = [dve.value_load(again_i[32 * q:32 * q + 1, 0:1], min_val=0, max_val=1) for q in range(P // 32)]
                with dve.If(left[0] + left[1] + left[2] + left[3] > 0):
                    with dve.Fori(0, NEWTON_MAX) as _:
                        dve.sem_clear(fix)
                        newton(h, 0, new_sum[:, :])

            def mark(b, part):
                dve.wait_ge(relu_done, H * b + 2 * G * (part + 1))
                nc.vector.tensor_scalar(flag[:, :], row_sum[:, 2 * G * part:2 * G * (part + 1)], 1.0 + SUM_TOL, None,
                                        ALU.is_gt).then_inc(flag_ready, 1)

            def settle(b, part):
                dve.sem_clear(check_step)
                dve.wait_ge(flag_sum, 2 * b + part + 1)
                nc.vector.tensor_scalar(flag_bits[:, :], flag_ps, 0.5, None, ALU.is_gt).then_inc(check_step, 1)
                dve.wait_ge(check_step, 1)
                nc.vector.scalar_tensor_tensor(flag_bits[:, :], flag_bits[:, :], 1.0, bit[:, :], ALU.mult, ALU.mult,
                                               accum_out=flag_code[:, :]).then_inc(check_step, 1)
                dve.wait_ge(check_step, 2)
                nc.vector.tensor_copy(flag_i[:, :], flag_code[:, :]).then_inc(check_step, 1)
                dve.wait_ge(check_step, 3)
                todo = dve.value_load(flag_i[0:1, 0:1], min_val=0, max_val=2 ** (2 * G) - 1)
                with dve.If(todo > 0):
                    for n in range(2 * G):
                        with dve.If((todo >> n) & 1 > 0):
                            refine(2 * G * part + n)
                dve.sem_inc(verified, 1)

            def tail1(b):
                def x1_of():
                    dve.wait_ge(att_ready, b + 1)
                    dve.wait_ge(res_ready, b + 1)
                    nc.vector.tensor_tensor(x1[:, :], att[:, :], xr[:, :], ALU.add).then_inc(x1_ready, 1)
                    dve.wait_ge(x1_ready, b + 1)
                layer_norm(b, x1, x1_of, st2, mv2, sd2, x2n, ln2_stat, ln2_sd, ln2_step, x2n_ready)

            def sum_squares(b):
                dve.wait_ge(sq_ready, b + 1)
                nc.vector.tensor_tensor(sq[:, 1, :], sq[:, 0, :], sq[:, 1, :], ALU.add).then_inc(sqsum_ready, 1)

            def tail2(b):
                dve.wait_ge(root_ready, b + 1)
                nc.vector.tensor_tensor(att[:, :], x1[:, :], sq[:, 0, :], ALU.add).then_inc(y_ready, 1)

            def angles(i, w, shift):
                n = [4 * i]
                turns = pT[:, :, :].rearrange("p g n -> p (g n)")[:, 0:DC * D].rearrange("p (c n) -> p c n", c=DC)

                def link(ins):
                    ins.then_inc(angle_step, 1)
                    n[0] += 1
                    dve.wait_ge(angle_step, n[0])

                n[0] = 8 * i
                link(nc.vector.tensor_tensor(w[:, :, :], w[:, :, :], v[:, 0:DC, :], ALU.add))
                link(nc.vector.tensor_scalar(turns, w[:, :, :], shift, 1.0 / TWO_PI, ALU.add, ALU.mult))
                link(nc.vector.tensor_scalar(turns, turns, ROUND, None, ALU.add))
                link(nc.vector.tensor_scalar(turns, turns, ROUND, None, ALU.subtract))
                link(nc.vector.scalar_tensor_tensor(w[:, :, :], turns, -TWO_PI_HI, w[:, :, :], ALU.mult, ALU.add))
                link(nc.vector.scalar_tensor_tensor(w[:, :, :], turns, -TWO_PI_LO, w[:, :, :], ALU.mult, ALU.add))
                link(nc.vector.tensor_scalar(w[:, :, :], w[:, :, :], shift, PI_BELOW, ALU.add, ALU.min))
                link(nc.vector.tensor_scalar(w[:, :, :], w[:, :, :], -PI_BELOW, None, ALU.max))
                dve.sem_inc(angle_ready, 1)

            nc.vector.memset(chain0[:, :, 1:TOP], 1.0)
            nc.vector.memset(chain0[:, :, 0:1], 0.0)
            nc.vector.memset(again[:, :], 0.0)
            for n in range(2 * G):
                nc.vector.memset(bit[:, n:n + 1], float(2 ** n))
            for k in range(TOP):
                last = nc.vector.memset(inv_k[:, :, k:k + 1], 1.0 / (k + 1))
            last.then_inc(dve_const, 1)
            nc.vector.memset(eps_c, LN_EPS).then_inc(dve_const, 2)
            dve.wait_ge(dve_const, 3)
            ln1(0)
            for n, (w2, heads, loaded) in enumerate(((wk2, slice(0, DC), in_wk), (wv2, slice(DC, 2 * DC), in_wv))):
                dve.wait_ge(loaded, 16)
                nc.vector.tensor_scalar(w2[:, 0, :, :], S[:, heads, 0:D], W_SCALE, None,
                                        ALU.mult).then_inc(weight_step, 1)
                dve.wait_ge(weight_step, n + 1)
                nc.vector.scalar_tensor_tensor(w2[:, 1, :, :], S[:, heads, 0:D], W_SCALE, w2[:, 0, :, :],
                                               ALU.mult, ALU.subtract).then_inc(split_ready, 1)
            ln1(1)
            dve.wait_ge(in_angle, 48)
            angles(0, wcos, TWO_PI / 4)
            dve.wait_ge(in_angle, 64)
            angles(1, wsin, 0.0)

            def one_pass(b, first, last):
                if not first:
                    mark(b - 1, 1)
                if not first and not last:
                    ln1(b + 1)
                if not first:
                    settle(b - 1, 1)
                thresholds(b, 0)
                thresholds(b, 1)
                thresholds(b, 2)
                if not first:
                    tail1(b - 1)
                mark(b, 0)
                thresholds(b, 3)
                if not first:
                    sum_squares(b - 1)
                settle(b, 0)
                if not first:
                    tail2(b - 1)

            passes(dve, one_pass)
            mark(B - 1, 1)
            settle(B - 1, 1)
            tail1(B - 1)
            sum_squares(B - 1)
            tail2(B - 1)


_INS = ["x", "ctx_1024", "L0_xattn_Wq", "L0_xattn_bq", "L0_xattn_Wk", "L0_xattn_bk", "L0_xattn_Wv", "L0_xattn_bv",
        "L0_xattn_Wo", "L0_xattn_bo", "L0_ffn_theta", "L0_ffn_phi", "L0_ffn_theta_noise", "L0_ffn_phi_noise"]


def kernel(**inputs):
    import numpy as np
    import concourse.bacc as bacc
    from concourse.bass_utils import run_bass_kernel_spmd

    nc = bacc.Bacc("TRN2", target_bir_lowering=False, num_devices=1)
    arrays, args = {}, []
    for name in _INS:
        a = np.ascontiguousarray(inputs[name])
        arrays[f"in_{name}"] = a
        args.append(nc.dram_tensor(f"in_{name}", a.shape, mybir.dt.from_np(a.dtype), kind="ExternalInput").ap())
    args.append(nc.dram_tensor("out_y", inputs["x"].shape, F32, kind="ExternalOutput").ap())
    build_kernel(nc, *args)
    r = run_bass_kernel_spmd(nc, [arrays], core_ids=[0])
    return r.results[0]["out_y"]
```
